# Optimizing a Trainium2 kernel written in Bass

```python
import numpy as np
import jax
import jax.numpy as jnp

def _softmax(x, axis=-1):
    return jax.nn.softmax(x, axis=axis)

def _gelu(x):
    return jax.nn.gelu(x, approximate=True)

def _silu(x):
    return jax.nn.silu(x)

def _sigmoid(x):
    return jax.nn.sigmoid(x)

def _layernorm(x, axis=-1, eps=1e-05):
    m = jnp.mean(x, axis=axis, keepdims=True)
    v = jnp.var(x, axis=axis, keepdims=True)
    return (x - m) / jnp.sqrt(v + eps)

def _scatter_add(tgt, idx, src, axis=0):
    return tgt.at[idx].add(src)

def _segment_sum(src, seg, n):
    return jax.ops.segment_sum(src, seg, n)
kernel_name = 'mk_xattn_seq_d1_seqx_r4_4a12cb'

def setup_inputs(seed: int=0):
    np.random.seed(seed)
    _w = jnp.asarray

    def _rec_inputs():
        import jax
        import jax.numpy as jnp
        _rk = jax.random.key(seed)
        x = -0.000296 + 1 * jax.random.normal(jax.random.fold_in(_rk, 1), (4, 512, 320), jnp.float32)
        _lenS = 512 - jax.random.randint(jax.random.fold_in(_rk, 7), (4,), 0, max(1, 512 // 4) + 1, jnp.int32)
        _lenS2 = 512 - jax.random.randint(jax.random.fold_in(_rk, 8), (4,), 0, max(1, 512 // 4) + 1, jnp.int32)
        _ctx_2048P = jax.random.normal(jax.random.fold_in(_rk, 11), (4, 16, 512), jnp.float32)
        _ctx_2048c = jax.random.dirichlet(jax.random.fold_in(_rk, 511), 0.3 * jnp.ones((16,), jnp.float32), (4, 512))
        _ctx_2048t = jnp.einsum('bsk,bkd->bsd', _ctx_2048c, _ctx_2048P)
        _ctx_2048t = _ctx_2048t * jax.lax.rsqrt(jnp.mean(jnp.square(_ctx_2048t)) + 1e-12) * 0.953939
        ctx_2048 = 0.00118529 + 0.99962 * (_ctx_2048t + 0.3 * jax.random.normal(jax.random.fold_in(_rk, 611), (4, 512, 512), jnp.float32))
        fside_Bx4x4_0 = jax.random.uniform(jax.random.fold_in(_rk, 12), (4, 4, 4), jnp.float32, 0.0, 0.981965)
        return (x, ctx_2048, fside_Bx4x4_0)
    x, ctx_2048, fside_Bx4x4_0 = _rec_inputs()

    def _L0_xattn_setup():
        import jax, jax.numpy as jnp
        import numpy as np
        HEADS = 20
        NUM_IP_TOKENS = 4
        NUM_DUMMY_TOKENS = 4
        IP_SCALE = 1.0
        ASPECT_RATIO = 1.0
        NEG = -10000.0

        def _grid_hw(seq_len, aspect_ratio):
            width = int((seq_len / aspect_ratio) ** 0.5)
            height = seq_len // width
            while width * height != seq_len:
                if width * height < seq_len:
                    width += 1
                else:
                    width -= 1
                height = seq_len // width
            return (height, width)

        def _sdpa(q, k, v, mask=None):
            dh = q.shape[-1]
            scores = jnp.einsum('bhqd,bhkd->bhqk', q, k) / jnp.sqrt(jnp.asarray(dh, q.dtype))
            if mask is not None:
                scores = scores + mask
            probs = jax.nn.softmax(scores, axis=-1)
            return jnp.einsum('bhqk,bhkd->bhqd', probs, v)

        def _split_heads(x, heads):
            b, l, d = x.shape
            return x.reshape(b, l, heads, d // heads).transpose(0, 2, 1, 3)

        def _merge_heads(x):
            b, h, l, dh = x.shape
            return x.transpose(0, 2, 1, 3).reshape(b, l, h * dh)

        def _ip_mask(bbox, batch_size, seq_len, dtype):
            M = bbox.shape[1]
            height, width = _grid_hw(seq_len, ASPECT_RATIO)
            x = jnp.linspace(0.0, 1.0, width, dtype=dtype)
            y = jnp.linspace(0.0, 1.0, height, dtype=dtype)
            yg, xg = jnp.meshgrid(y, x, indexing='ij')
            xg = xg.reshape(-1)
            yg = yg.reshape(-1)
            x1, y1, x2, y2 = (bbox[..., 0:1], bbox[..., 1:2], bbox[..., 2:3], bbox[..., 3:4])
            inside = (xg >= x1) & (xg <= x2) & (yg >= y1) & (yg <= y2)
            ip_mask = jnp.where(inside, 0.0, NEG).astype(dtype)
            ip_mask = jnp.transpose(ip_mask, (0, 2, 1))[:, None]
            ip_mask = jnp.repeat(ip_mask, NUM_IP_TOKENS // M, axis=-1)
            dummy = jnp.where(jnp.any(inside, axis=1), NEG, 0.0).astype(dtype)
            dummy = jnp.repeat(dummy[:, None, :, None], NUM_DUMMY_TOKENS, axis=-1)
            return jnp.concatenate([dummy, ip_mask], axis=-1)
        key = jax.random.key(seed)
        ks = jax.random.split(key, 12)
        B, S, D, C = (4, 1024, 320, 512)
        text_len, M = (77, 4)
        hidden_states = jax.random.normal(ks[0], (B, S, D), jnp.float32)
        encoder_hidden_states = jax.random.normal(ks[1], (B, text_len + NUM_IP_TOKENS + NUM_DUMMY_TOKENS, C), jnp.float32)
        p1 = jax.random.uniform(ks[2], (B, M, 2), jnp.float32)
        p2 = jax.random.uniform(ks[3], (B, M, 2), jnp.float32)
        bbox = jnp.concatenate([jnp.minimum(p1, p2), jnp.maximum(p1, p2)], axis=-1)
        s = 0.02
        w_q = jax.random.normal(ks[4], (D, D), jnp.float32) * s
        w_k = jax.random.normal(ks[5], (C, D), jnp.float32) * s
        w_v = jax.random.normal(ks[6], (C, D), jnp.float32) * s
        w_k_ip = jax.random.normal(ks[7], (C, D), jnp.float32) * s
        w_v_ip = jax.random.normal(ks[8], (C, D), jnp.float32) * s
        w_out = jax.random.normal(ks[9], (D, D), jnp.float32) * s
        b_out = jnp.zeros((D,), jnp.float32)
        return {'hidden_states': hidden_states, 'encoder_hidden_states': encoder_hidden_states, 'bbox': bbox, 'w_q': w_q, 'w_k': w_k, 'w_v': w_v, 'w_k_ip': w_k_ip, 'w_v_ip': w_v_ip, 'w_out': w_out, 'b_out': b_out}
    _L0_xattn_all = _L0_xattn_setup()
    _L0_xattn_in = {k: v for k, v in _L0_xattn_all.items() if k in ('w_q', 'w_k', 'w_v', 'w_k_ip', 'w_v_ip', 'w_out', 'b_out')}
    del _L0_xattn_all
    return {'x': x, 'ctx_2048': ctx_2048, 'fside_Bx4x4_0': fside_Bx4x4_0, 'L0_xattn_w_q': _L0_xattn_in['w_q'], 'L0_xattn_w_k': _L0_xattn_in['w_k'], 'L0_xattn_w_v': _L0_xattn_in['w_v'], 'L0_xattn_w_k_ip': _L0_xattn_in['w_k_ip'], 'L0_xattn_w_v_ip': _L0_xattn_in['w_v_ip'], 'L0_xattn_w_out': _L0_xattn_in['w_out'], 'L0_xattn_b_out': _L0_xattn_in['b_out']}

def reference(x, ctx_2048, fside_Bx4x4_0, L0_xattn_w_q, L0_xattn_w_k, L0_xattn_w_v, L0_xattn_w_k_ip, L0_xattn_w_v_ip, L0_xattn_w_out, L0_xattn_b_out):
    import jax
    import jax.numpy as jnp

    def _L0_xattn_ref(hidden_states, encoder_hidden_states, bbox, w_q, w_k, w_v, w_k_ip, w_v_ip, w_out, b_out):
        import jax, jax.numpy as jnp
        import numpy as np
        HEADS = 20
        NUM_IP_TOKENS = 4
        NUM_DUMMY_TOKENS = 4
        IP_SCALE = 1.0
        ASPECT_RATIO = 1.0
        NEG = -10000.0

        def _grid_hw(seq_len, aspect_ratio):
            width = int((seq_len / aspect_ratio) ** 0.5)
            height = seq_len // width
            while width * height != seq_len:
                if width * height < seq_len:
                    width += 1
                else:
                    width -= 1
                height = seq_len // width
            return (height, width)

        def _sdpa(q, k, v, mask=None):
            dh = q.shape[-1]
            scores = jnp.einsum('bhqd,bhkd->bhqk', q, k) / jnp.sqrt(jnp.asarray(dh, q.dtype))
            if mask is not None:
                scores = scores + mask
            probs = jax.nn.softmax(scores, axis=-1)
            return jnp.einsum('bhqk,bhkd->bhqd', probs, v)

        def _split_heads(x, heads):
            b, l, d = x.shape
            return x.reshape(b, l, heads, d // heads).transpose(0, 2, 1, 3)

        def _merge_heads(x):
            b, h, l, dh = x.shape
            return x.transpose(0, 2, 1, 3).reshape(b, l, h * dh)

        def _ip_mask(bbox, batch_size, seq_len, dtype):
            M = bbox.shape[1]
            height, width = _grid_hw(seq_len, ASPECT_RATIO)
            x = jnp.linspace(0.0, 1.0, width, dtype=dtype)
            y = jnp.linspace(0.0, 1.0, height, dtype=dtype)
            yg, xg = jnp.meshgrid(y, x, indexing='ij')
            xg = xg.reshape(-1)
            yg = yg.reshape(-1)
            x1, y1, x2, y2 = (bbox[..., 0:1], bbox[..., 1:2], bbox[..., 2:3], bbox[..., 3:4])
            inside = (xg >= x1) & (xg <= x2) & (yg >= y1) & (yg <= y2)
            ip_mask = jnp.where(inside, 0.0, NEG).astype(dtype)
            ip_mask = jnp.transpose(ip_mask, (0, 2, 1))[:, None]
            ip_mask = jnp.repeat(ip_mask, NUM_IP_TOKENS // M, axis=-1)
            dummy = jnp.where(jnp.any(inside, axis=1), NEG, 0.0).astype(dtype)
            dummy = jnp.repeat(dummy[:, None, :, None], NUM_DUMMY_TOKENS, axis=-1)
            return jnp.concatenate([dummy, ip_mask], axis=-1)
        B, S, D = hidden_states.shape
        residual = hidden_states
        end_pos = encoder_hidden_states.shape[1] - (NUM_IP_TOKENS + NUM_DUMMY_TOKENS)
        text = encoder_hidden_states[:, :end_pos]
        ip_h = encoder_hidden_states[:, end_pos:]
        q = _split_heads(hidden_states @ w_q, HEADS)
        k = _split_heads(text @ w_k, HEADS)
        v = _split_heads(text @ w_v, HEADS)
        out_text = _sdpa(q, k, v)
        out_text = _merge_heads(out_text)
        mask_ip = _ip_mask(bbox, B, S, hidden_states.dtype)
        k_ip = _split_heads(ip_h @ w_k_ip, HEADS)
        v_ip = _split_heads(ip_h @ w_v_ip, HEADS)
        out_ip = _merge_heads(_sdpa(q, k_ip, v_ip, mask=mask_ip))
        out = out_text + IP_SCALE * out_ip
        out = out @ w_out + b_out
        out = out + residual
        return out
    x = _L0_xattn_ref(x, ctx_2048, fside_Bx4x4_0, L0_xattn_w_q, L0_xattn_w_k, L0_xattn_w_v, L0_xattn_w_k_ip, L0_xattn_w_v_ip, L0_xattn_w_out, L0_xattn_b_out)
    return x

_drawn_inputs = setup_inputs


def setup_inputs(seed=0):
    import zlib

    import numpy as np

    out = dict(_drawn_inputs(seed))
    spreads = {'L0_xattn_b_out': (0.0, 0.1)}
    factors = {'L0_xattn_w_q': 6.026, 'L0_xattn_w_k': 8.0, 'L0_xattn_w_k_ip': 6.802}
    for name, (base, spread) in spreads.items():
        noise = np.random.default_rng([zlib.crc32(name.encode()), seed]).standard_normal(out[name].shape)
        drawn = base * np.exp(spread * noise) if base else spread * noise
        out[name] = jnp.asarray(drawn.astype(out[name].dtype))
    for name, factor in factors.items():
        out[name] = (out[name] * factor).astype(out[name].dtype)
    return out
```

```python
import concourse.bass as bass
from concourse import mybir
from contextlib import ExitStack


def cross_attention_kernel(
    nc: bass.Bass,
    x: bass.AP,
    ctx_in: bass.AP,
    bbox: bass.AP,
    w_q: bass.AP,
    w_k: bass.AP,
    w_v: bass.AP,
    w_k_ip: bass.AP,
    w_v_ip: bass.AP,
    w_out: bass.AP,
    b_out: bass.AP,
    grid: bass.AP,
    eye: bass.AP,
    out: bass.AP,
):
    fp32 = mybir.dt.float32
    bf16 = mybir.dt.bfloat16
    ALU = mybir.AluOpType
    ACT = mybir.ActivationFunctionType
    AX = mybir.AxisListType

    B, S, D = x.shape
    C = ctx_in.shape[2]
    H, DH, NIP = 20, D // 20, 8
    T = ctx_in.shape[1] - NIP
    NEG = -10000.0
    GH = 4
    NG = H // GH
    NT = 4
    QT, KT = S // NT, T // NT
    HT = 128 // DH
    NC = C // 128
    TILES = [(t, min(128, D - 128 * t)) for t in range((D + 127) // 128)]
    ND = len(TILES)
    PAIRS = [(0, 0), (1, 0), (2, 0), (0, 1), (1, 1), (0, 2), (1, 2)]
    SR = DH * len(PAIRS)
    STEPS, SLOTS = NG * NT, GH
    UNITS = STEPS * SLOTS
    LEAD = 6
    SCALE = float(DH) ** -0.5

    PLAN = {
        (0, 0): ("xt", 0), (0, 1): ("xt", 1), (0, 2): ("xt", 2), (0, 3): ("ct", 0),
        (1, 0): ("ct", 1), (1, 1): ("ct", 2), (1, 2): ("ct", 3), (1, 3): ("pt", 0),
        (2, 0): ("pt", 1), (2, 1): ("mt", 1), (2, 2): ("q", 0), (2, 3): ("ips", 1),
        (3, 0): ("oip", 0), (3, 1): ("oip", 1), (3, 2): ("k", 0), (3, 3): ("oip", 2),
        (4, 0): ("f", 0), (4, 2): ("f", 1), (5, 0): ("f", 2), (5, 2): ("f", 3),
        (6, 1): ("mt", 2), (6, 2): ("q", 1), (6, 3): ("ips", 2), (7, 1): ("k", 1),
        (8, 1): ("v", 0), (9, 1): ("q", 2), (10, 1): ("mt", 3), (10, 3): ("ips", 3),
        (11, 1): ("k", 2), (12, 1): ("v", 1), (13, 1): ("v", 2), (14, 1): ("mt", 4),
        (14, 3): ("ips", 4), (15, 1): ("v", 3), (18, 1): ("mt", 0), (18, 3): ("ips", 0),
    }
    NEXT = ("xt", "ct", "q", "k", "v")
    LAST = ("pt", "oip", "f")
    PROLOGUE = ([("xt", i) for i in range(ND)] + [("ct", i) for i in range(NC)]
                + [("q", 0), ("k", 0), ("cit", 0), ("kip", 0), ("vip", 0),
                   ("q", 1), ("k", 1), ("q", 2), ("k", 2)]
                + [("v", i) for i in range(NT)] + [("mt", 0), ("ips", 0)])
    EPILOGUE = ([("pt", 0), ("pt", 1)] + [("oip", i) for i in range(ND)]
                + [("f", i) for i in range(NT)])

    def plan(has_last, has_next):
        def kept(task):
            if task[0] in NEXT or task in (("mt", 0), ("ips", 0)):
                return has_next
            return has_last or task[0] not in LAST
        return {at: task for at, task in PLAN.items() if kept(task)}

    class Turns:

        def __init__(self, tasks, half, odd):
            self.place = {task: n for n, task in enumerate(tasks)}
            self.half, self.odd, self.count = half, odd, len(tasks)

        def has(self, task):
            return task in self.place

        def bank(self, task):
            return (self.place[task] + self.odd) % 2

        def uses(self, task):
            return self.half + (self.place[task] + self.odd) // 2

        def done(self, task):
            return self.half * 2 + self.odd + self.place[task] + 1

    N0 = len(PROLOGUE)
    N1 = len(plan(False, True))
    NB = len(PLAN)
    assert NB % 2 == 0

    def turns(b, has_last, has_next):
        tasks = [plan(has_last, has_next)[at] for at in sorted(plan(has_last, has_next))]
        if not has_last:
            return Turns(tasks, N0 // 2, N0 % 2)
        return Turns(tasks, (N0 + N1) // 2 + (b - 1) * (NB // 2), (N0 + N1) % 2)

    PRO = Turns(PROLOGUE, 0, 0)
    before_end = N0 + N1 + (B - 2) * NB + len(plan(True, False))
    EPI = Turns(EPILOGUE, before_end // 2, before_end % 2)

    ctx = ExitStack()
    with ctx:
        def sb(name, shape, dt=fp32):
            return ctx.enter_context(nc.sbuf_tensor(name, shape, dt))

        def pb(name):
            return ctx.enter_context(nc.psum_tensor(name, [128, 512], fp32))

        def sem(name):
            return ctx.enter_context(nc.semaphore(name))

        wq = sb("wq", [128, ND, D])
        wk = sb("wk", [128, NC, D])
        wv = sb("wv", [128, NC, D])
        wo = sb("wo", [128, ND, D])
        bias = sb("bias", [128, D])
        idf = sb("idf", [128, 128])
        idb = sb("idb", [128, 128], bf16)
        xs = sb("xs", [128, NT, D])
        cs = sb("cs", [KT, NT, C])
        xT = sb("xT", [128, ND, S])
        cT = sb("cT", [128, NC, T])
        parts = sb("parts", [128, 2, ND, 3, S], bf16)
        resid = sb("resid", [128, 2, S])
        qst = sb("qst", [128, H, S], bf16)
        kst = sb("kst", [128, H, T], bf16)
        vst = sb("vst", [KT, NT, D])
        vaug = sb("vaug", [KT, NT, H, 2 * DH])
        mrow = sb("mrow", [128, GH * NT])
        mres = sb("mres", [128, GH * NT])
        mparts = sb("mparts", [128, 3 * GH * NT], bf16)
        mT = sb("mT", [3 * GH * NT, 128], bf16)
        P = sb("P", [KT, 2, GH, S])
        og = sb("og", [128, 2, S])
        num = sb("num", [128, ND, S])
        den = sb("den", [128, ND, S])
        oT = sb("oT", [128, ND, S])
        xres = sb("xres", [128, NT, D])
        ob = sb("ob", [128, NT, D])
        cip = sb("cip", [B * NIP, C])
        cipT = sb("cipT", [128, NC, B * NIP])
        kipr = sb("kipr", [128, ND, B * NIP])
        kipp = sb("kipp", [128, 3, ND, B * NIP], bf16)
        kipst = sb("kipst", [SR, H, B * NIP], bf16)
        vips = sb("vips", [B * NIP, D])
        vblocks = sb("vblocks", [128, B, ND, 128])
        vb = sb("vb", [128, ND, 128])
        ips = sb("ips", [128, NT, H * NIP])
        ipp = sb("ipp", [128, NT, H * NIP])
        ipmax = sb("ipmax", [128, NT * H])
        ipden = sb("ipden", [128, NT * H])
        pT = sb("pT", [128, 2, S])
        boxes = sb("boxes", [128, B, 4, 4])
        gxy = sb("gxy", [128, NT, 2])
        cmp = sb("cmp", [128, 4, B * NT * 4])
        anyin = sb("anyin", [128, B * NT])
        mask = sb("mask", [128, B, NT, NIP])

        parts_d = nc.dram_tensor("parts_scratch", [2, ND, 3, 128, S], bf16, kind="Internal").ap()
        kip_d = nc.dram_tensor("kip_scratch", [3, ND, 128, B * NIP], bf16, kind="Internal").ap()
        vip_d = nc.dram_tensor("vip_scratch", [B * NIP, D], fp32, kind="Internal").ap()
        og_d = nc.dram_tensor("og_scratch", [NG, GH, 2, DH, S], fp32, kind="Internal").ap()

        st_bank = [pb(f"st_bank{i}") for i in range(2)]
        mx_bank = [pb(f"mx_bank{i}") for i in range(2)]
        pv_bank = [pb(f"pv_bank{i}") for i in range(2)]
        work = [pb(f"work{i}") for i in range(2)]

        x_in, c_in, xres_in = sem("x_in"), sem("c_in"), sem("xres_in")
        wq_in, wk_in, wv_in, wo_in = sem("wq_in"), sem("wk_in"), sem("wv_in"), sem("wo_in")
        wip_in, eye_in, box_in, cip_in, bias_in = (sem("wip_in"), sem("eye_in"), sem("box_in"),
                                                   sem("cip_in"), sem("bias_in"))
        zeroed_v, zeroed_p, idb_made = sem("zeroed_v"), sem("zeroed_p"), sem("idb_made")
        work_done = sem("work_done")
        work_free = [sem(f"work_free{i}") for i in range(2)]
        first_part = sem("first_part")
        parts_made = sem("parts_made")
        parts_out = [sem(f"parts_out{t}") for t in range(ND)]
        stacked = [sem(f"stacked{t}") for t in range(ND)]
        values_made = sem("values_made")
        mx_done, mx_read = sem("mx_done"), sem("mx_read")
        m_step, m_parts = sem("m_step"), sem("m_parts")
        m_rows = sem("m_rows")
        st_done, exp_done, pv_done = sem("st_done"), sem("exp_done"), sem("pv_done")
        og_made, og_out = sem("og_made"), sem("og_out")
        placed = [sem(f"placed{t}") for t in range(ND)]
        den_inv, normed = sem("den_inv"), sem("normed")
        kip_first, kip_step, kip_parts, kip_out, kip_in = (sem("kip_first"), sem("kip_step"),
                                                           sem("kip_parts"), sem("kip_out"), sem("kip_in"))
        vip_out, vblocks_in, vb_made = sem("vip_out"), sem("vblocks_in"), sem("vb_made")
        box_step, mask_made = sem("box_step"), sem("mask_made")
        ip_masked, ip_max, ip_shifted, ip_exp, ip_step, ip_inv, ip_probs = (
            sem("ip_masked"), sem("ip_max"), sem("ip_shifted"), sem("ip_exp"), sem("ip_step"),
            sem("ip_inv"), sem("ip_probs"))
        res_made, stored, cut_step = sem("res_made"), sem("stored"), sem("cut_step")


        wip = sb("wip", [128, NC, D])

        block = ctx.enter_context(nc.Block())

        @block.sync
        def _(sp):
            def load_inputs(b):
                sp.dma_start(xs[:, :, :], x[b].rearrange("(n p) d -> p n d", p=QT)).then_inc(x_in, 16)
                sp.dma_start(cs[:, :, :], ctx_in[b, 0:T].rearrange("(n p) c -> p n c", p=KT)).then_inc(c_in, 16)

            def store_parts(t, rows, b):
                sp.wait_ge(parts_made, 2 * ND * b + 2 * t + 2)
                if b is not None and not (isinstance(b, int) and b == 0):
                    sp.wait_ge(stacked[t], 16 * 2 * len(PAIRS) * b)
                for kind, width in ((0, S), (1, T)):
                    sp.dma_start(parts_d[kind, t, :, 0:rows, 0:width].rearrange("i r s -> r i s"),
                                 parts[0:rows, kind, t, :, 0:width]).then_inc(parts_out[t], 16)

            def fill_stacks(t, rows, b, units_done):
                sp.wait_ge(parts_out[t], 32 * (b + 1))
                if units_done is None:
                    sp.wait_ge(zeroed_v, 6)
                else:
                    sp.wait_ge(st_done, units_done)
                for kind, stack, width in ((0, qst, S), (1, kst, T)):
                    for slot, pair in enumerate(PAIRS):
                        sp.dma_start(
                            stack[slot * DH:(slot + 1) * DH, t * HT:t * HT + rows // DH, :],
                            parts_d[kind, t, pair[kind], 0:rows, 0:width].rearrange("(h d) s -> d h s", d=DH),
                        ).then_inc(stacked[t], 16)

            def put_maxima(n, g, tn):
                sp.wait_ge(work_free[tn.bank(("mt", g))], tn.uses(("mt", g)) + 1)
                for i in range(3):
                    sp.dma_start(qst[SR + i:SR + i + 1, g * GH:(g + 1) * GH, :].rearrange("o h s -> o (h s)"),
                                 mT[i * GH * NT:(i + 1) * GH * NT, :]).then_inc(m_rows, 16)

            def place_output(b, g):
                n = NG * b + g
                sp.wait_ge(og_made, n + 1)
                if not (isinstance(b, int) and b == 0):
                    sp.wait_ge(stored, 16 * NT * b)
                sp.dma_start(og_d[g].rearrange("j c d s -> (j c d) s"), og[:, g % 2]).then_inc(og_out, 16)
                sp.wait_ge(og_out, 16 * (n + 1))
                t, r = g // 2, (g % 2) * GH * DH
                for c, dst in ((0, num), (1, den)):
                    for j in range(1):
                        sp.dma_start(dst[r:r + GH * DH, t, :], og_d[g, :, c]).then_inc(placed[t], 16)

            def load_residual(b):
                sp.dma_start(xres[:, :, :], x[b].rearrange("(n p) d -> p n d", p=QT)).then_inc(xres_in, 16)

            def store_output(b, i, tn):
                sp.wait_ge(work_free[tn.bank(("f", i))], tn.uses(("f", i)) + 1)
                sp.dma_start(out[b, i * QT:(i + 1) * QT], ob[:, i]).then_inc(stored, 16)

            def iteration(b, has_last, has_next):
                tn = turns(b, has_last, has_next)
                for s in range(STEPS):
                    if s == 0 and has_last:
                        place_output(b - 1, NG - 1)
                        fill_stacks(2, TILES[2][1], b, UNITS * b)
                    if s == 1 and has_next and not (isinstance(b, int) and b == B - 2):
                        sp.wait_ge(work_done, tn.done(("ct", NC - 1)))
                        load_inputs(b + 2)
                    if s % 4 == 3 and (has_next or s < STEPS - 1):
                        g = (s + 1) // 4 % NG
                        put_maxima(0, g, tn)
                    if s == 5 and has_next:
                        store_parts(0, 128, b + 1)
                    if has_last and s in (4, 5):
                        store_output(b - 1, 2 * (s - 4), tn)
                        store_output(b - 1, 2 * (s - 4) + 1, tn)
                    if s == 6:
                        load_residual(b)
                    if s == 8 and has_next:
                        fill_stacks(0, 128, b + 1, UNITS * b + 32)
                    if s == 9 and has_next:
                        store_parts(1, 128, b + 1)
                    if s == 13 and has_next:
                        store_parts(2, TILES[2][1], b + 1)
                    if s % 4 == 2 and s > 4:
                        place_output(b, s // 4 - 1)
                    if s == 16 and has_next:
                        fill_stacks(1, 128, b + 1, UNITS * b + 64)

            sp.dma_start(idf[:, :], eye).then_inc(eye_in, 16)
            load_inputs(0)
            for t in range(ND):
                rows = TILES[t][1]
                sp.dma_start(wq[0:rows, t, :], w_q[128 * t:128 * t + rows]).then_inc(wq_in, 16)
            sp.dma_start(cip[:, :], ctx_in[:, T:T + NIP, :]).then_inc(cip_in, 16)
            for t in range(ND):
                rows = TILES[t][1]
                sp.dma_start(wo[0:rows, t, :], w_out[128 * t:128 * t + rows]).then_inc(wo_in, 16)
            sp.dma_start(bias[:, :], b_out.unsqueeze(0).broadcast_to([128, D])).then_inc(bias_in, 16)
            sp.dma_start(boxes[:, :, :, :].rearrange("p b m c -> p (b m c)"),
                         bbox.rearrange("b m c -> (b m c)").unsqueeze(0).broadcast_to([128, B * 16])).then_inc(box_in, 16)
            sp.dma_start(gxy[:, :, :], grid.rearrange("(n p) c -> p n c", p=QT)).then_inc(box_in, 16)
            for t, rows in TILES:
                store_parts(t, rows, 0)
                fill_stacks(t, rows, 0, None)
                if t == 0:
                    sp.wait_ge(kip_parts, 1)
                    for i in range(3):
                        for tt, rr in TILES:
                            sp.dma_start(kip_d[i, tt, 0:rr], kipp[0:rr, i, tt]).then_inc(kip_out, 16)
                    sp.wait_ge(work_free[PRO.bank(("vip", 0))], PRO.uses(("vip", 0)) + 1)
                    sp.dma_start(vip_d, vips[:, :]).then_inc(vip_out, 16)
                    sp.wait_ge(kip_out, 16 * 3 * ND)
                    for slot, pair in enumerate(PAIRS):
                        for tt, rr in TILES:
                            sp.dma_start(kipst[slot * DH:(slot + 1) * DH, tt * HT:tt * HT + rr // DH, :],
                                         kip_d[pair[1], tt, 0:rr].rearrange("(h d) m -> d h m", d=DH)).then_inc(kip_in, 16)
                    sp.wait_ge(vip_out, 16)
                    sp.wait_ge(zeroed_p, 2)
                    for h in range(H):
                        tt, r = h // HT, h % (2 * HT) * NIP
                        sp.dma_start(vblocks[r:r + NIP, :, tt, h % HT * DH:(h % HT + 1) * DH],
                                     vip_d.rearrange("(b k) c -> k b c", k=NIP)[:, :, h * DH:(h + 1) * DH]).then_inc(vblocks_in, 16)
            sp.wait_ge(work_done, PRO.done(("ct", NC - 1)))
            load_inputs(1)
            put_maxima(0, 0, PRO)

            iteration(0, False, True)
            for b in range(1, B - 1):
                iteration(b, True, True)
            iteration(B - 1, True, False)
            place_output(B - 1, NG - 1)
            for i in range(NT):
                store_output(B - 1, i, EPI)
            sp.wait_ge(stored, 16 * NT * B)
            for t in range(ND):
                sp.wait_ge(stacked[t], 16 * 2 * len(PAIRS) * B)

        @block.tensor
        def _(pe):
            def taken(task, tn):
                pe.wait_ge(work_free[tn.bank(task)], tn.uses(task) + 1)

            def task(which, b, tn):
                kind, i = which
                bank = work[tn.bank(which)]
                uses = tn.uses(which)
                if not (isinstance(uses, int) and uses == 0):
                    pe.wait_ge(work_free[tn.bank(which)], uses)
                if kind == "xt":
                    if i == 0:
                        pe.wait_ge(x_in, 16 * (b + 1))
                    rows = TILES[i][1]
                    for n in range(NT):
                        last = nc.tensor.transpose(bank[0:rows, n * QT:(n + 1) * QT],
                                                   xs[:, n, 128 * i:128 * i + rows], idf[:, :])
                elif kind == "ct":
                    if i == 0:
                        pe.wait_ge(c_in, 16 * (b + 1))
                    for n in range(NT):
                        last = nc.tensor.transpose(bank[:, n * KT:(n + 1) * KT],
                                                   cs[:, n, 128 * i:128 * (i + 1)], idf[0:KT, 0:KT])
                elif kind == "q":
                    if i == 0:
                        taken(("xt", ND - 1), tn)
                        taken(("xt", ND - 2), tn)
                    for c in range(ND):
                        last = nc.tensor.matmul(bank[0:TILES[i][1], :], wq[:, c, 128 * i:128 * i + TILES[i][1]],
                                                xT[:, c, :], start=(c == 0), stop=(c == ND - 1))
                elif kind == "k":
                    if i == 0:
                        taken(("ct", NC - 1), tn)
                        taken(("ct", NC - 2), tn)
                    for c in range(NC):
                        last = nc.tensor.matmul(bank[0:TILES[i][1], 0:T], wk[:, c, 128 * i:128 * i + TILES[i][1]],
                                                cT[:, c, :], start=(c == 0), stop=(c == NC - 1))
                elif kind == "v":
                    for c in range(NC):
                        last = nc.tensor.matmul(bank[0:KT, 0:D], cT[:, c, i * KT:(i + 1) * KT], wv[:, c, :],
                                                start=(c == 0), stop=(c == NC - 1))
                elif kind == "mt":
                    pe.wait_ge(m_parts, NG * b + i + 1)
                    last = nc.tensor.transpose(bank[:, :].bitcast(bf16)[0:3 * GH * NT, 0:128], mparts[:, :], idb[:, :])
                elif kind == "ips":
                    for n in range(NT):
                        for j in range(GH):
                            h = i * GH + j
                            last = nc.tensor.matmul(bank[:, (n * GH + j) * NIP:(n * GH + j + 1) * NIP],
                                                    qst[0:SR, h, n * QT:(n + 1) * QT],
                                                    kipst[:, h, NIP * b:NIP * b + NIP],
                                                    start=True, stop=True)
                elif kind == "pt":
                    pe.wait_ge(ip_probs, b + 1)
                    cols = min(128, H * NIP - 128 * i)
                    for n in range(NT):
                        last = nc.tensor.transpose(bank[0:cols, n * QT:(n + 1) * QT],
                                                   ipp[:, n, 128 * i:128 * i + cols], idf[:, :])
                elif kind == "oip":
                    if i == 0:
                        taken(("pt", 0), tn)
                        taken(("pt", 1), tn)
                        pe.wait_ge(vb_made, b + 1)
                    last = nc.tensor.matmul(bank[0:TILES[i][1], :], vb[:, i, 0:TILES[i][1]], pT[:, i // 2, :],
                                            start=True, stop=True)
                elif kind == "f":
                    if i == 0:
                        for t in range(ND):
                            taken(("oip", t), tn)
                    for t in range(ND):
                        last = nc.tensor.matmul(bank[:, 0:D], oT[:, t, i * QT:(i + 1) * QT], wo[:, t, :],
                                                start=(t == 0), stop=(t == ND - 1))
                elif kind == "cit":
                    pe.wait_ge(cip_in, 16)
                    for c in range(NC):
                        last = nc.tensor.transpose(bank[:, c * B * NIP:(c + 1) * B * NIP],
                                                   cip[:, 128 * c:128 * (c + 1)], idf[0:B * NIP, 0:B * NIP])
                elif kind == "kip":
                    taken(("cit", 0), tn)
                    pe.wait_ge(wip_in, 16)
                    for t, rows in TILES:
                        for c in range(NC):
                            last = nc.tensor.matmul(bank[0:rows, t * B * NIP:(t + 1) * B * NIP],
                                                    wip[:, c, 128 * t:128 * t + rows], cipT[:, c, :],
                                                    start=(c == 0), stop=(c == NC - 1))
                elif kind == "vip":
                    pe.wait_ge(wip_in, 32)
                    for c in range(NC):
                        last = nc.tensor.matmul(bank[0:B * NIP, 0:D], cipT[:, c, :], wip[:, c, :],
                                                start=(c == 0), stop=(c == NC - 1))
                last.then_inc(work_done, 1)

            def st(b, s, j):
                g, kt = s // NT, s % NT
                h = g * GH + j
                i = UNITS * b + s * SLOTS + j
                if kt == 0 and j == 0:
                    pe.wait_ge(m_rows, 48 * (NG * b + g + 1))
                if not (isinstance(i, int) and i < 2):
                    pe.wait_ge(exp_done, i - 1)
                nc.tensor.matmul(st_bank[j % 2][0:KT, :], kst[:, h, kt * KT:(kt + 1) * KT], qst[:, h, :],
                                 start=True, stop=True).then_inc(st_done, 1)

            def mx(b, u, j):
                g, n = u // NT, u % NT
                h = g * GH + j
                i = UNITS * b + u * SLOTS + j
                if n == 0 and j == 0 and g % 2 == 0:
                    pe.wait_ge(stacked[g // 2], 16 * 2 * len(PAIRS) * (b + 1))
                if not (isinstance(i, int) and i < 2):
                    pe.wait_ge(mx_read, i - 1)
                nc.tensor.matmul(mx_bank[j % 2][:, 0:T], qst[0:SR, h, n * QT:(n + 1) * QT], kst[0:SR, h, :],
                                 start=True, stop=True).then_inc(mx_done, 1)

            def pv(b, s):
                g, kt = s // NT, s % NT
                if kt == 0:
                    pe.wait_ge(values_made, NG * b + g + 1)
                    earlier = NG * b + g - {0: 1, 1: 3}.get(g, 2)
                    if not (isinstance(earlier, int) and earlier < 0):
                        pe.wait_ge(og_made, earlier + 1)
                pe.wait_ge(exp_done, UNITS * b + (s + 1) * SLOTS)
                for j in range(GH):
                    last = nc.tensor.matmul(pv_bank[g % 2][32 * j:32 * (j + 1), :], vaug[:, kt, g * GH + j, :],
                                            P[:, s % 2, j, :], start=(kt == 0), stop=(kt == NT - 1))
                last.then_inc(pv_done, 1)

            def iteration(b, has_last, has_next):
                tn = turns(b, has_last, has_next)
                tasks = plan(has_last, has_next)
                for s in range(STEPS):
                    for j in range(SLOTS):
                        st(b, s, j)
                        u = s + LEAD
                        if u < STEPS:
                            mx(b, u, j)
                        elif has_next:
                            mx(b + 1, u - STEPS, j)
                        if (s, j) in tasks:
                            which = tasks[s, j]
                            kind = which[0]
                            of = b + 1 if kind in NEXT or which in (("mt", 0), ("ips", 0)) else b - 1 if kind in LAST else b
                            task(which, of, tn)
                        if j == 1 and s > 0:
                            pv(b, s - 1)
                pv(b, STEPS - 1)

            pe.wait_ge(eye_in, 16)
            pe.wait_ge(zeroed_v, 4)
            pe.wait_ge(wq_in, 16 * ND)
            for which in PROLOGUE:
                if which == ("k", 0):
                    pe.wait_ge(wk_in, 16)
                if which == ("v", 0):
                    pe.wait_ge(wv_in, 16)
                if which == ("mt", 0):
                    for u in range(NT):
                        for j in range(SLOTS):
                            mx(0, u, j)
                    pe.wait_ge(idb_made, 1)
                if which == ("ips", 0):
                    pe.wait_ge(kip_in, 16 * ND * len(PAIRS))
                    pe.wait_ge(wo_in, 16 * ND)
                task(which, 0, PRO)
            for u in range(NT, LEAD):
                for j in range(SLOTS):
                    mx(0, u, j)
            iteration(0, False, True)
            for b in range(1, B - 1):
                iteration(b, True, True)
            iteration(B - 1, True, False)
            for which in EPILOGUE:
                task(which, B - 1, EPI)

        @block.scalar
        def _(act):
            def copy_out(dst, src, which, tn):
                nc.scalar.activation(dst, src, ACT.Copy).then_inc(work_free[tn.bank(which)], 1)

            def task(which, b, tn):
                kind, i = which
                if kind in ("oip", "f"):
                    return
                bank = work[tn.bank(which)]
                act.wait_ge(work_done, tn.done(which))
                if kind == "xt":
                    rows = TILES[i][1]
                    copy_out(xT[0:rows, i, :], bank[0:rows, :], which, tn)
                elif kind == "ct":
                    copy_out(cT[:, i, :], bank[:, 0:T], which, tn)
                elif kind in ("q", "k"):
                    rows, width = TILES[i][1], S if kind == "q" else T
                    if not (isinstance(b, int) and b == 0):
                        act.wait_ge(parts_out[i], 32 * b)
                    nc.scalar.activation(parts[0:rows, "qk".index(kind), i, 0, 0:width], bank[0:rows, 0:width],
                                         ACT.Copy).then_inc(first_part, 1)
                elif kind == "v":
                    if i == 0 and not (isinstance(b, int) and b == 0):
                        act.wait_ge(values_made, NG * b)
                    copy_out(vst[:, i, :], bank[0:KT, 0:D], which, tn)
                elif kind == "mt":
                    n = NG * b + i
                    if not (isinstance(n, int) and n == 0):
                        act.wait_ge(m_rows, 48 * n)
                    copy_out(mT[:, :], bank[:, :].bitcast(bf16)[0:3 * GH * NT, 0:128], which, tn)
                elif kind == "ips":
                    if not (isinstance(b, int) and b == 0):
                        act.wait_ge(ip_masked, b)
                    nc.scalar.activation(ips[:, :, i * GH * NIP:(i + 1) * GH * NIP],
                                         bank[:, 0:NT * GH * NIP].rearrange("p (n c) -> p n c", n=NT),
                                         ACT.Copy, scale=SCALE).then_inc(work_free[tn.bank(which)], 1)
                elif kind == "pt":
                    cols = min(128, H * NIP - 128 * i)
                    copy_out(pT[0:cols, i, :], bank[0:cols, :], which, tn)
                elif kind == "cit":
                    copy_out(cipT[:, :, :].rearrange("p c m -> p (c m)"), bank[:, 0:NC * B * NIP], which, tn)
                elif kind == "kip":
                    for t, rows in TILES:
                        nc.scalar.activation(kipp[0:rows, 0, t], bank[0:rows, t * B * NIP:(t + 1) * B * NIP],
                                             ACT.Copy).then_inc(kip_first, 1)
                elif kind == "vip":
                    copy_out(vips[:, :], bank[0:B * NIP, 0:D], which, tn)

            def exp(b, s, j):
                i = UNITS * b + s * SLOTS + j
                act.wait_ge(st_done, i + 1)
                step = STEPS * b + s
                if j == 0 and not (isinstance(step, int) and step < 2):
                    act.wait_ge(pv_done, step - 1)
                nc.scalar.activation(P[:, s % 2, j, :], st_bank[j % 2][0:KT, :], ACT.Exp,
                                     scale=SCALE).then_inc(exp_done, 1)

            def take_output(b, g):
                n = NG * b + g
                act.wait_ge(pv_done, NT * (n + 1))
                earlier = n - {0: 1, 1: 3}.get(g, 2)
                if not (isinstance(earlier, int) and earlier < 0):
                    act.wait_ge(og_out, 16 * (earlier + 1))
                nc.scalar.activation(og[:, g % 2, :], pv_bank[g % 2][:, :], ACT.Copy).then_inc(og_made, 1)

            def iteration(b, has_last, has_next):
                tn = turns(b, has_last, has_next)
                tasks = plan(has_last, has_next)
                for s in range(STEPS):
                    for j in range(SLOTS):
                        exp(b, s, j)
                        if (s, j) in tasks:
                            which = tasks[s, j]
                            kind = which[0]
                            of = b + 1 if kind in NEXT or which in (("mt", 0), ("ips", 0)) else b - 1 if kind in LAST else b
                            task(which, of, tn)
                        if j == 2 and s > 0 and s % NT == 0:
                            take_output(b, s // NT - 1)
                        if (s, j) == (17, 0):
                            act.wait_ge(ip_shifted, b + 1)
                            nc.scalar.activation(ipp[:, :, :], ipp[:, :, :], ACT.Exp).then_inc(ip_exp, 1)
                take_output(b, NG - 1)

            act.dma_start(wk[:, :, :], w_k.rearrange("(c p) d -> p c d", p=128)).then_inc(wk_in, 16)
            act.dma_start(wip[:, :, :], w_k_ip.rearrange("(c p) d -> p c d", p=128)).then_inc(wip_in, 16)
            act.dma_start(wv[:, :, :], w_v.rearrange("(c p) d -> p c d", p=128)).then_inc(wv_in, 16)
            for which in PROLOGUE:
                if which == ("vip", 0):
                    act.wait_ge(work_done, PRO.done(("kip", 0)))
                    act.dma_start(wip[:, :, :], w_v_ip.rearrange("(c p) d -> p c d", p=128)).then_inc(wip_in, 16)
                task(which, 0, PRO)
            iteration(0, False, True)
            for b in range(1, B - 1):
                iteration(b, True, True)
            iteration(B - 1, True, False)
            for which in EPILOGUE:
                task(which, B - 1, EPI)

        @block.vector
        def _(dve):
            def task(which, b, tn):
                kind, i = which
                if kind not in ("q", "k", "oip", "f", "kip"):
                    return
                bank = work[tn.bank(which)]
                free = work_free[tn.bank(which)]
                if kind in ("q", "k"):
                    n = 2 * ND * b + 2 * i + "qk".index(kind)
                    rows, width = TILES[i][1], S if kind == "q" else T
                    dve.wait_ge(first_part, n + 1)
                    if not (isinstance(n, int) and n < 2):
                        dve.wait_ge(parts_made, n - 1)
                    nc.vector.tensor_tensor(resid[0:rows, "qk".index(kind), 0:width], bank[0:rows, 0:width],
                                            parts[0:rows, "qk".index(kind), i, 0, 0:width],
                                            ALU.subtract).then_inc(free, 1)
                elif kind == "oip":
                    rows = TILES[i][1]
                    dve.wait_ge(work_done, tn.done(which))
                    dve.wait_ge(normed, ND * b + i + 1)
                    nc.vector.tensor_tensor(oT[0:rows, i, :], bank[0:rows, :], num[0:rows, i, :],
                                            ALU.add).then_inc(free, 1)
                elif kind == "f":
                    dve.wait_ge(work_done, tn.done(which))
                    if i == 0:
                        dve.wait_ge(res_made, b + 1)
                        if not (isinstance(b, int) and b == 0):
                            dve.wait_ge(stored, 16 * NT * b)
                    nc.vector.tensor_tensor(ob[:, i, :], bank[:, 0:D], xres[:, i, :], ALU.add).then_inc(free, 1)
                elif kind == "kip":
                    w = B * NIP
                    dve.wait_ge(kip_first, ND)
                    for t, rows in TILES:
                        nc.vector.tensor_tensor(kipr[0:rows, t], bank[0:rows, t * w:(t + 1) * w],
                                                kipp[0:rows, 0, t], ALU.subtract).then_inc(kip_step, 1)
                    dve.wait_ge(kip_step, ND)
                    for t, rows in TILES:
                        nc.vector.tensor_copy(kipp[0:rows, 1, t], kipr[0:rows, t]).then_inc(kip_step, 1)
                    dve.wait_ge(kip_step, 2 * ND)
                    for t, rows in TILES:
                        last = nc.vector.tensor_tensor(kipp[0:rows, 2, t], kipr[0:rows, t], kipp[0:rows, 1, t], ALU.subtract)
                        if t < ND - 1:
                            last.then_inc(kip_step, 1)
                    last.then_inc(kip_parts, 1)
                    dve.wait_ge(kip_parts, 1)
                    nc.vector.memset(kipr[0:1, 0, 0:1], 0.0).then_inc(free, 1)

            def row_max(b, u, j):
                n = u % NT
                i = UNITS * b + u * SLOTS + j
                dve.wait_ge(mx_done, i + 1)
                nc.vector.tensor_reduce(mrow[:, j * NT + n:j * NT + n + 1], mx_bank[j % 2][:, 0:T],
                                        axis=AX.X, op=ALU.max).then_inc(mx_read, 1)

            def cut_maxima(b, g):
                n = NG * b + g
                w = GH * NT
                dve.wait_ge(mx_read, UNITS * b + (g + 1) * NT * SLOTS)
                nc.vector.tensor_scalar(mparts[:, 0:w], mrow[:, :], -1.0, None, ALU.mult).then_inc(m_step, 1)
                dve.wait_ge(m_step, 3 * n + 1)
                nc.vector.scalar_tensor_tensor(out=mres[:, :], in0=mrow[:, :], scalar=-1.0, in1=mparts[:, 0:w],
                                               op0=ALU.mult, op1=ALU.subtract).then_inc(m_step, 1)
                dve.wait_ge(m_step, 3 * n + 2)
                nc.vector.tensor_copy(mparts[:, w:2 * w], mres[:, :]).then_inc(m_step, 1)
                dve.wait_ge(m_step, 3 * n + 3)
                nc.vector.tensor_tensor(mparts[:, 2 * w:3 * w], mres[:, :], mparts[:, w:2 * w],
                                        ALU.subtract).then_inc(m_parts, 1)

            def invert_den(b, t):
                rows = TILES[t][1]
                dve.wait_ge(placed[t], (b + 1) * (64 if t < 2 else 32))
                nc.vector.reciprocal(den[0:rows, t, :], den[0:rows, t, :]).then_inc(den_inv, 1)

            def iteration(b, has_last, has_next):
                tn = turns(b, has_last, has_next)
                tasks = plan(has_last, has_next)
                for s in range(STEPS):
                    for j in range(SLOTS):
                        u = s + LEAD
                        if u < STEPS:
                            row_max(b, u, j)
                        elif has_next:
                            row_max(b + 1, u - STEPS, j)
                        if j == SLOTS - 1 and s % NT == 1:
                            if u < STEPS:
                                cut_maxima(b, u // NT)
                            elif has_next:
                                cut_maxima(b + 1, u // NT - NG)
                        if (s, j) in tasks:
                            which = tasks[s, j]
                            kind = which[0]
                            of = b + 1 if kind in NEXT or which in (("mt", 0), ("ips", 0)) else b - 1 if kind in LAST else b
                            task(which, of, tn)
                        if (s, j) == (2, 0) and has_last:
                            invert_den(b - 1, 2)
                        if (s, j) == (12, 0):
                            invert_den(b, 0)
                        if (s, j) == (19, 0):
                            invert_den(b, 1)
                        if (s, j) == (16, 0):
                            dve.wait_ge(ip_masked, b + 1)
                            nc.vector.tensor_reduce(ipmax[:, :], ipp[:, :, :].rearrange("p n (h k) -> p (n h) k", k=NIP),
                                                    axis=AX.X, op=ALU.max).then_inc(ip_max, 1)
                        if (s, j) == (18, 0):
                            dve.wait_ge(ip_exp, b + 1)
                            nc.vector.tensor_reduce(ipden[:, :], ipp[:, :, :].rearrange("p n (h k) -> p (n h) k", k=NIP),
                                                    axis=AX.X, op=ALU.add).then_inc(ip_step, 1)
                            dve.wait_ge(ip_step, b + 1)
                            nc.vector.reciprocal(ipden[:, :], ipden[:, :]).then_inc(ip_inv, 1)

            for padded in (xT, wq, wo, oT):
                nc.vector.memset(padded[TILES[-1][1]:128, ND - 1, :], 0.0).then_inc(zeroed_v, 1)
            nc.vector.memset(qst[96:128, :, :].rearrange("p h s -> p (h s)"), 0.0).then_inc(zeroed_v, 1)
            nc.vector.memset(kst[96:128, :, :].rearrange("p h s -> p (h s)"), 1.0).then_inc(zeroed_v, 1)
            dve.wait_ge(eye_in, 16)
            nc.vector.tensor_copy(idb[:, :], idf[:, :]).then_inc(idb_made, 1)
            dve.wait_ge(box_in, 32)
            for e, (corner, axis, op) in enumerate(((0, 0, ALU.is_ge), (1, 1, ALU.is_ge), (2, 0, ALU.is_le), (3, 1, ALU.is_le))):
                for b in range(B):
                    nc.vector.tensor_tensor(
                        cmp[:, e, 16 * b:16 * (b + 1)].rearrange("p (n m) -> p n m", n=NT),
                        gxy[:, :, axis:axis + 1].broadcast_to([128, NT, 4]),
                        boxes[:, b, :, corner].unsqueeze(1).broadcast_to([128, NT, 4]), op).then_inc(box_step, 1)
            dve.wait_ge(box_step, 4 * B)
            nc.vector.tensor_tensor(cmp[:, 0], cmp[:, 0], cmp[:, 1], ALU.mult).then_inc(box_step, 1)
            nc.vector.tensor_tensor(cmp[:, 2], cmp[:, 2], cmp[:, 3], ALU.mult).then_inc(box_step, 1)
            dve.wait_ge(box_step, 4 * B + 2)
            nc.vector.tensor_tensor(cmp[:, 0], cmp[:, 0], cmp[:, 2], ALU.mult).then_inc(box_step, 1)
            dve.wait_ge(box_step, 4 * B + 3)
            inside = cmp[:, 0].rearrange("p (n m) -> p n m", m=4)
            nc.vector.tensor_reduce(anyin[:, :], inside, axis=AX.X, op=ALU.max).then_inc(box_step, 1)
            mask_rows = mask[:, :, :, :].rearrange("p b n k -> p (b n) k")
            nc.vector.tensor_scalar(mask_rows[:, :, 4:8], inside, 1.0, -NEG, ALU.subtract, ALU.mult).then_inc(mask_made, 1)
            dve.wait_ge(box_step, 4 * B + 4)
            nc.vector.tensor_scalar(mask_rows[:, :, 0:4], anyin[:, :].unsqueeze(2).broadcast_to([128, B * NT, 4]),
                                    NEG, None, ALU.mult).then_inc(mask_made, 1)
            for which in PROLOGUE:
                if which == ("mt", 0):
                    for u in range(NT):
                        for j in range(SLOTS):
                            row_max(0, u, j)
                    cut_maxima(0, 0)
                task(which, 0, PRO)
            for u in range(NT, LEAD):
                for j in range(SLOTS):
                    row_max(0, u, j)
            iteration(0, False, True)
            for b in range(1, B - 1):
                iteration(b, True, True)
            iteration(B - 1, True, False)
            invert_den(B - 1, 2)
            for which in EPILOGUE:
                task(which, B - 1, EPI)

        @block.gpsimd
        def _(pool):
            def cut(kind, t, b, tn):
                which = ("qk"[kind], t)
                rows, width = TILES[t][1], (S, T)[kind]
                pool.wait_ge(work_free[tn.bank(which)], tn.uses(which) + 1)
                if not (isinstance(b, int) and b == 0):
                    pool.wait_ge(parts_out[t], 32 * b)
                n = 2 * ND * b + 2 * t + kind
                nc.gpsimd.tensor_copy(parts[0:rows, kind, t, 1, 0:width], resid[0:rows, kind, 0:width]).then_inc(cut_step, 1)
                pool.wait_ge(cut_step, n + 1)
                nc.gpsimd.tensor_tensor(out=parts[0:rows, kind, t, 2, 0:width], in0=resid[0:rows, kind, 0:width],
                                        in1=parts[0:rows, kind, t, 1, 0:width], op=ALU.subtract).then_inc(parts_made, 1)

            def lay_values(b, g, tn):
                if g == 0:
                    for i in (NT - 2, NT - 1):
                        pool.wait_ge(work_free[tn.bank(("v", i))], tn.uses(("v", i)) + 1)
                if not (isinstance(b, int) and b == 0):
                    pool.wait_ge(pv_done, STEPS * (b - 1) + NT * (g + 1))
                nc.gpsimd.tensor_copy(
                    vaug[:, :, g * GH:(g + 1) * GH, 0:DH],
                    vst[:, :, g * GH * DH:(g + 1) * GH * DH].rearrange("p n (h d) -> p n h d", d=DH)).then_inc(values_made, 1)

            def normalise(b, t):
                rows = TILES[t][1]
                pool.wait_ge(den_inv, ND * b + t + 1)
                nc.gpsimd.tensor_tensor(out=num[0:rows, t], in0=num[0:rows, t], in1=den[0:rows, t],
                                        op=ALU.mult).then_inc(normed, 1)

            def add_bias(b):
                pool.wait_ge(xres_in, 16 * (b + 1))
                nc.gpsimd.tensor_tensor(out=xres[:, :, :], in0=xres[:, :, :],
                                        in1=bias[:, :].unsqueeze(1).broadcast_to([128, NT, D]),
                                        op=ALU.add).then_inc(res_made, 1)

            heads = ipp[:, :, :].rearrange("p n (h k) -> p (n h) k", k=NIP)

            def mask_scores(b, tn):
                pool.wait_ge(work_free[tn.bank(("ips", 4))], tn.uses(("ips", 4)) + 1)
                if tn.has(("pt", 1)):
                    pool.wait_ge(work_done, tn.done(("pt", 1)))
                for n in range(NT):
                    last = nc.gpsimd.tensor_tensor(
                        out=ipp[:, n].rearrange("p (h k) -> p h k", k=NIP),
                        in0=ips[:, n].rearrange("p (h k) -> p h k", k=NIP),
                        in1=mask[:, b, n, :].unsqueeze(1).broadcast_to([128, H, NIP]), op=ALU.add)
                last.then_inc(ip_masked, 1)

            def shift(b):
                pool.wait_ge(ip_max, b + 1)
                nc.gpsimd.tensor_tensor(out=heads, in0=heads, in1=ipmax[:, :].unsqueeze(2).broadcast_to([128, NT * H, NIP]),
                                        op=ALU.subtract).then_inc(ip_shifted, 1)

            def probabilities(b):
                pool.wait_ge(ip_inv, b + 1)
                nc.gpsimd.tensor_tensor(out=heads, in0=heads, in1=ipden[:, :].unsqueeze(2).broadcast_to([128, NT * H, NIP]),
                                        op=ALU.mult).then_inc(ip_probs, 1)

            def lay_ip_values(b, tn):
                if tn.has(("oip", 2)):
                    pool.wait_ge(work_done, tn.done(("oip", 2)))
                nc.gpsimd.tensor_copy(vb[:, :, :], vblocks[:, b, :, :]).then_inc(vb_made, 1)

            def iteration(b, has_last, has_next):
                tn = turns(b, has_last, has_next)
                if has_last:
                    lay_values(b, NG - 1, None)
                    add_bias(b - 1)
                    normalise(b - 1, 2)
                if has_next:
                    for t in range(ND):
                        cut(0, t, b + 1, tn)
                        cut(1, t, b + 1, tn)
                normalise(b, 0)
                lay_ip_values(b, tn)
                mask_scores(b, tn)
                if has_next:
                    for g in range(3):
                        lay_values(b + 1, g, tn)
                shift(b)
                if has_next:
                    lay_values(b + 1, 3, tn)
                probabilities(b)
                normalise(b, 1)


            nc.gpsimd.memset(vblocks[:, :, :, :].rearrange("p b t c -> p (b t c)"), 0.0).then_inc(zeroed_p, 1)
            nc.gpsimd.memset(pT[:, 1, :], 0.0).then_inc(zeroed_p, 1)
            pool.wait_ge(zeroed_p, 2)
            nc.gpsimd.memset(vaug[:, :, :, :].rearrange("p n h c -> p (n h c)"), 1.0).then_inc(zeroed_p, 1)
            pool.wait_ge(zeroed_p, 3)
            for t in range(ND):
                cut(0, t, 0, PRO)
                cut(1, t, 0, PRO)
            for g in range(NG):
                lay_values(0, g, PRO)
            pool.wait_ge(vblocks_in, 16 * H)
            pool.wait_ge(bias_in, 16)
            pool.wait_ge(mask_made, 2)
            iteration(0, False, True)
            for b in range(1, B - 1):
                iteration(b, True, True)
            iteration(B - 1, True, False)
            add_bias(B - 1)
            normalise(B - 1, 2)


_INS = ['x', 'ctx_2048', 'fside_Bx4x4_0', 'L0_xattn_w_q', 'L0_xattn_w_k', 'L0_xattn_w_v',
        'L0_xattn_w_k_ip', 'L0_xattn_w_v_ip', 'L0_xattn_w_out', 'L0_xattn_b_out']


def kernel(**inputs):
    import numpy as _np
    import concourse.bacc as _bacc
    from concourse import mybir as _mybir
    from concourse.bass_utils import run_bass_kernel_spmd as _run

    nc = _bacc.Bacc("TRN2", target_bir_lowering=False, num_devices=1)
    arrays, args = {}, []

    def give(name, a):
        arrays[name] = a
        args.append(nc.dram_tensor(name, a.shape, _mybir.dt.from_np(a.dtype), kind="ExternalInput").ap())

    for name in _INS:
        give(f"in_{name}_dram", _np.ascontiguousarray(inputs[name]))
    seq = inputs['x'].shape[1]
    width = next(w for w in range(int(seq ** 0.5), seq + 1) if seq % w == 0)

    def line(n):
        c = _np.arange(n, dtype=_np.float32) * (_np.float32(1) / _np.float32(n - 1))
        c[-1] = 1
        return c
    pos = _np.arange(seq)
    grid = _np.stack([line(width)[pos % width], line(seq // width)[pos // width]], axis=1)
    give("grid_dram", _np.ascontiguousarray(grid))
    give("eye_dram", _np.eye(128, dtype=_np.float32))
    shape = tuple(inputs['x'].shape)
    args.append(nc.dram_tensor("out_0_dram", shape, _mybir.dt.float32, kind="ExternalOutput").ap())
    cross_attention_kernel(nc, *args)
    r = _run(nc, [arrays], core_ids=[0])
    return r.results[0]["out_0_dram"]
```

```python
import concourse.bass as bass
from concourse import mybir
from contextlib import ExitStack


def cross_attention_kernel(
    nc: bass.Bass,
    x: bass.AP,
    x_t: bass.AP,
    ctx_t: bass.AP,
    ctx_ip_t: bass.AP,
    bbox: bass.AP,
    w_q: bass.AP,
    w_k: bass.AP,
    w_v: bass.AP,
    w_k_ip: bass.AP,
    w_v_ip: bass.AP,
    w_out: bass.AP,
    b_out: bass.AP,
    grid: bass.AP,
    eye: bass.AP,
    out: bass.AP,
):
    fp32 = mybir.dt.float32
    bf16 = mybir.dt.bfloat16
    ALU = mybir.AluOpType
    ACT = mybir.ActivationFunctionType
    AX = mybir.AxisListType

    B, S, D = x.shape
    C = ctx_t.shape[1]
    H, DH, NIP = 20, D // 20, 8
    T = ctx_t.shape[2] - NIP
    NEG = -10000.0
    GH = 4
    NG = H // GH
    NT = 4
    QT, KT = S // NT, T // NT
    HT = 128 // DH
    NC = C // 128
    TILES = [(t, min(128, D - 128 * t)) for t in range((D + 127) // 128)]
    ND = len(TILES)
    PAIRS = [(0, 0), (1, 0), (2, 0), (0, 1), (1, 1), (0, 2), (1, 2)]
    SR = DH * len(PAIRS)
    STEPS, SLOTS = NG * NT, GH
    UNITS = STEPS * SLOTS
    LEAD = 6
    SCALE = float(DH) ** -0.5

    PLAN = {
        (0, 3): ("q", 0), (1, 1): ("pt", 0), (1, 3): ("k", 0), (2, 2): ("mt", 1), (2, 3): ("ips", 1),
        (3, 1): ("q", 1), (4, 1): ("pt", 1), (4, 3): ("k", 1), (5, 1): ("oip", 0), (6, 2): ("mt", 2),
        (6, 3): ("ips", 2), (7, 1): ("qk", 2), (7, 3): ("oip", 1), (8, 2): ("oip", 2),
        (9, 1): ("v", 0), (10, 2): ("mt", 3), (10, 1): ("f", 0), (10, 3): ("ips", 3),
        (11, 1): ("v", 1), (12, 2): ("f", 1), (13, 1): ("v", 2), (14, 2): ("mt", 4),
        (14, 3): ("ips", 4), (15, 1): ("v", 3), (16, 1): ("f", 2), (18, 2): ("mt", 0),
        (18, 3): ("ips", 0), (19, 3): ("f", 3),
    }
    FIRST = {(3, 3): ("vip", 0), (5, 1): ("ips_first", 0)}
    NEXT = ("q", "k", "qk", "v")
    LAST = ("pt", "oip", "f")
    PROLOGUE = ([("q", 0), ("k", 0), ("q", 1), ("k", 1), ("qk", 2), ("kip", 0)]
                + [("v", i) for i in range(NT)] + [("mt", 0)])
    EPILOGUE = ([("pt", 0), ("pt", 1)] + [("oip", i) for i in range(ND)]
                + [("f", i) for i in range(NT)])
    PROJ = [("q", 0), ("k", 0), ("q", 1), ("k", 1), ("qk", 2)]
    NP = len(PROJ)

    def plan(has_last, has_next):
        def kept(task):
            if task[0] in NEXT or task in (("mt", 0), ("ips", 0)):
                return has_next
            return has_last or task[0] not in LAST
        kept_tasks = {at: task for at, task in PLAN.items() if kept(task)}
        if not has_last:
            kept_tasks.update(FIRST)
            kept_tasks[5, 3] = kept_tasks.pop((2, 3))
        return kept_tasks

    def batch_of(task, b):
        if task[0] in NEXT or task in (("mt", 0), ("ips", 0)):
            return b + 1
        return b - 1 if task[0] in LAST else b

    class Turns:

        def __init__(self, tasks, half, odd):
            self.place = {task: n for n, task in enumerate(tasks)}
            self.half, self.odd, self.count = half, odd, len(tasks)

        def has(self, task):
            return task in self.place

        def bank(self, task):
            return (self.place[task] + self.odd) % 2

        def uses(self, task):
            return self.half + (self.place[task] + self.odd) // 2

        def done(self, task):
            return self.half * 2 + self.odd + self.place[task] + 1

    N0 = len(PROLOGUE)
    N1 = len(plan(False, True))
    NB = len(PLAN)
    assert NB % 2 == 0

    def turns(b, has_last, has_next):
        tasks = [plan(has_last, has_next)[at] for at in sorted(plan(has_last, has_next))]
        if not has_last:
            return Turns(tasks, N0 // 2, N0 % 2)
        return Turns(tasks, (N0 + N1) // 2 + (b - 1) * (NB // 2), (N0 + N1) % 2)

    PRO = Turns(PROLOGUE, 0, 0)
    before_end = N0 + N1 + (B - 2) * NB + len(plan(True, False))
    EPI = Turns(EPILOGUE, before_end // 2, before_end % 2)

    ctx = ExitStack()
    with ctx:
        def sb(name, shape, dt=fp32):
            return ctx.enter_context(nc.sbuf_tensor(name, shape, dt))

        def pb(name):
            return ctx.enter_context(nc.psum_tensor(name, [128, 512], fp32))

        def sem(name):
            return ctx.enter_context(nc.semaphore(name))

        wq = sb("wq", [128, ND, D])
        wk = sb("wk", [128, NC, D])
        wv = sb("wv", [128, NC, D])
        wo = sb("wo", [128, ND, D])
        bias = sb("bias", [128, D])
        idf = sb("idf", [128, 128])
        idb = sb("idb", [128, 128], bf16)
        xT = sb("xT", [128, ND, S])
        cT = sb("cT", [128, NC, T + NIP])
        parts = sb("parts", [128, NP, 3, S], bf16)
        resid = sb("resid", [128, 2, S])
        qst = sb("qst", [128, H, S], bf16)
        kst = sb("kst", [128, H, T], bf16)
        vst = sb("vst", [KT, NT, D])
        vaug = sb("vaug", [KT, NT, H, 2 * DH])
        mrow = sb("mrow", [128, GH * NT])
        mres = sb("mres", [128, GH * NT])
        mparts = sb("mparts", [128, 3 * GH * NT], bf16)
        mT = sb("mT", [3 * GH * NT, 128], bf16)
        P = sb("P", [KT, 2, GH, S])
        og = sb("og", [128, 2, S])
        num = sb("num", [128, ND, S])
        den = sb("den", [128, ND, S])
        denc = sb("denc", [128, 2, GH * S // 128])
        oT = sb("oT", [128, ND, S])
        xres = sb("xres", [128, NT, D])
        ob = sb("ob", [128, NT, D])
        cipT = sb("cipT", [128, NC, B * NIP])
        kipr = sb("kipr", [128, ND, B * NIP])
        kipp = sb("kipp", [128, 3, ND, B * NIP], bf16)
        kipst = sb("kipst", [SR, H, B * NIP], bf16)
        vips = sb("vips", [B * NIP, D])
        vblocks = sb("vblocks", [128, B, ND, 128])
        vb = sb("vb", [128, ND, 128])
        ips = sb("ips", [128, NT, H * NIP])
        ipp = sb("ipp", [128, NT, H * NIP])
        ipmax = sb("ipmax", [128, NT * H])
        ipden = sb("ipden", [128, NT * H])
        pT = sb("pT", [128, 2, S])
        boxes = sb("boxes", [128, B, 4, 4])
        gxy = sb("gxy", [128, NT, 2])
        cmp = sb("cmp", [128, 4, B * NT * 4])
        anyin = sb("anyin", [128, B * NT])
        mask = sb("mask", [128, B, NT, NIP])

        parts_d = nc.dram_tensor("parts_scratch", [NP, 3, 128, S], bf16, kind="Internal").ap()
        kip_d = nc.dram_tensor("kip_scratch", [3, D, B * NIP], bf16, kind="Internal").ap()
        vip_d = nc.dram_tensor("vip_scratch", [B * NIP, D], fp32, kind="Internal").ap()
        den_d = nc.dram_tensor("den_scratch", [NG, GH, S], fp32, kind="Internal").ap()
        og_d = nc.dram_tensor("og_scratch", [NG, GH, 2, DH, S], fp32, kind="Internal").ap()

        st_bank = [pb(f"st_bank{i}") for i in range(2)]
        mx_bank = [pb(f"mx_bank{i}") for i in range(2)]
        pv_bank = [pb(f"pv_bank{i}") for i in range(2)]
        work = [pb(f"work{i}") for i in range(2)]

        x_in, c_in, xres_in = sem("x_in"), sem("c_in"), sem("xres_in")
        wq_in, wk_in, wv_in, wo_in = sem("wq_in"), sem("wk_in"), sem("wv_in"), sem("wo_in")
        wip_in, eye_in, box_in, cip_in, bias_in = (sem("wip_in"), sem("eye_in"), sem("box_in"),
                                                   sem("cip_in"), sem("bias_in"))
        zeroed_v, zeroed_p, idb_made = sem("zeroed_v"), sem("zeroed_p"), sem("idb_made")
        work_done = sem("work_done")
        work_free = [sem(f"work_free{i}") for i in range(2)]
        first_part = sem("first_part")
        parts_made = sem("parts_made")
        second_part = sem("second_part")
        parts_out = [sem(f"parts_out{i}") for i in range(NP)]
        stacked = [sem(f"stacked{t}") for t in range(ND)]
        values_made = sem("values_made")
        mx_done, mx_read = sem("mx_done"), sem("mx_read")
        m_step, m_parts = sem("m_step"), sem("m_parts")
        m_rows = sem("m_rows")
        st_done, exp_done, pv_done = sem("st_done"), sem("exp_done"), sem("pv_done")
        og_made, og_out = sem("og_made"), sem("og_out")
        placed = [sem(f"placed{t}") for t in range(ND)]
        den_in, den_inv, den_out, normed = sem("den_in"), sem("den_inv"), sem("den_out"), sem("normed")
        kip_first, kip_step, kip_parts, kip_out, kip_in = (sem("kip_first"), sem("kip_step"),
                                                           sem("kip_parts"), sem("kip_out"), sem("kip_in"))
        vip_out, vblocks_in, vb_made = sem("vip_out"), sem("vblocks_in"), sem("vb_made")
        box_step, mask_made = sem("box_step"), sem("mask_made")
        ip_masked, ip_max, ip_shifted, ip_exp, ip_step, ip_inv, ip_probs = (
            sem("ip_masked"), sem("ip_max"), sem("ip_shifted"), sem("ip_exp"), sem("ip_step"),
            sem("ip_inv"), sem("ip_probs"))
        res_made, stored = sem("res_made"), sem("stored")


        wip = sb("wip", [128, NC, D])

        block = ctx.enter_context(nc.Block())

        @block.sync
        def _(sp):
            def load_x(b):
                for t, rows in TILES:
                    sp.dma_start(xT[0:rows, t, :], x_t[b, 128 * t:128 * t + rows]).then_inc(x_in, 16)

            def load_ctx(b):
                sp.dma_start(cT[:, :, :], ctx_t[b].rearrange("(c p) n -> p c n", p=128)).then_inc(c_in, 16)

            def store_parts(i, b):
                sp.wait_ge(parts_made, NP * b + i + 1)
                if not (isinstance(b, int) and b == 0):
                    sp.wait_ge(stacked[i // 2], 16 * 2 * len(PAIRS) * b)
                sp.dma_start(parts_d[i].rearrange("i r s -> r i s"), parts[:, i]).then_inc(parts_out[i], 16)

            def fill_stack(kind, t, b, units_done, slots=range(len(PAIRS))):
                rows = TILES[t][1]
                tile, r = (2 * t + kind, 0) if rows == 128 else (NP - 1, kind * rows)
                stack, width = (qst, S) if kind == 0 else (kst, T)
                sp.wait_ge(parts_out[tile], 16 * (b + 1))
                if units_done is None:
                    sp.wait_ge(zeroed_p, 2)
                else:
                    sp.wait_ge(st_done, units_done)
                for slot in slots:
                    pair = PAIRS[slot]
                    sp.dma_start(
                        stack[slot * DH:(slot + 1) * DH, t * HT:t * HT + rows // DH, :],
                        parts_d[tile, pair[kind], r:r + rows, 0:width].rearrange("(h d) s -> d h s", d=DH),
                    ).then_inc(stacked[t], 16)

            def fill_stacks(t, b, units_done):
                fill_stack(0, t, b, units_done)
                fill_stack(1, t, b, units_done)

            def put_maxima(g, tn):
                which = ("mt", g)
                sp.wait_ge(work_free[tn.bank(which)], tn.uses(which) + 1)
                sp.dma_start(qst[SR:SR + 3, g * GH:(g + 1) * GH, :].rearrange("i h s -> i (h s)"),
                             mT[:, :]).then_inc(m_rows, 16)

            def place_output(b, g, tn=None):
                n = NG * b + g
                sp.wait_ge(og_made, n + 1)
                read = ("oip", g // 2)
                if g % 2 == 0 and tn is not None and tn.has(read):
                    sp.wait_ge(work_free[tn.bank(read)], tn.uses(read) + 1)
                sp.dma_start(og_d[g].rearrange("j c d s -> (j c d) s"), og[:, g % 2]).then_inc(og_out, 16)
                sp.wait_ge(og_out, 16 * (n + 1))
                t, r = g // 2, (g % 2) * GH * DH
                sp.dma_start(denc[:, g % 2, :], og_d[g, :, 1, 0].rearrange("j (r w) -> j r w", r=128 // GH)).then_inc(den_in, 16)
                sp.dma_start(num[r:r + GH * DH, t, :], og_d[g, :, 0]).then_inc(placed[t], 16)

            def spread_den(b, g):
                n = NG * b + g
                t, r = g // 2, (g % 2) * GH * DH
                sp.wait_ge(den_inv, n + 1)
                sp.dma_start(den_d[g].rearrange("j (r w) -> j r w", r=128 // GH), denc[:, g % 2, :]).then_inc(den_out, 16)
                sp.wait_ge(den_out, 16 * (n + 1))
                sp.dma_start(den[r:r + GH * DH, t, :],
                             den_d[g].unsqueeze(1).broadcast_to([GH, DH, S])).then_inc(placed[t], 16)

            def load_residual(b):
                sp.dma_start(xres[:, :, :], x[b].rearrange("(n p) d -> p n d", p=QT)).then_inc(xres_in, 16)

            def store_output(b, i, tn):
                sp.wait_ge(work_free[tn.bank(("f", i))], tn.uses(("f", i)) + 1)
                sp.dma_start(out[b, i * QT:(i + 1) * QT], ob[:, i]).then_inc(stored, 16)

            def stack_ip_keys():
                sp.wait_ge(kip_parts, 1)
                for t, rows in TILES:
                    sp.dma_start(kip_d[:, 128 * t:128 * t + rows].rearrange("i r m -> r i m"),
                                 kipp[0:rows, :, t]).then_inc(kip_out, 16)
                sp.wait_ge(kip_out, 16 * ND)
                for slot, pair in enumerate(PAIRS):
                    sp.dma_start(kipst[slot * DH:(slot + 1) * DH, :, :],
                                 kip_d[pair[1]].rearrange("(h d) m -> d h m", d=DH)).then_inc(kip_in, 16)

            def store_ip_values(tn):
                sp.wait_ge(work_free[tn.bank(("vip", 0))], tn.uses(("vip", 0)) + 1)
                sp.dma_start(vip_d, vips[:, :]).then_inc(vip_out, 16)

            def lay_blocks():
                sp.wait_ge(vip_out, 16)
                sp.wait_ge(zeroed_p, 3)
                for h in range(H):
                    t, r = h // HT, h % (2 * HT) * NIP
                    sp.dma_start(vblocks[r:r + NIP, :, t, h % HT * DH:(h % HT + 1) * DH],
                                 vip_d.rearrange("(b k) c -> k b c", k=NIP)[:, :, h * DH:(h + 1) * DH]).then_inc(vblocks_in, 16)

            def iteration(b, has_last, has_next):
                tn = turns(b, has_last, has_next)
                for s in range(STEPS):
                    if s % 4 == 2 and tn.has(("mt", (s + 2) // 4 % NG)):
                        put_maxima((s + 2) // 4 % NG, tn)
                    if s == 0 and has_last:
                        place_output(b - 1, NG - 1)
                    if s == 1 and has_last:
                        fill_stacks(2, b, UNITS * b)
                    if s == 2 and has_last:
                        spread_den(b - 1, NG - 1)
                    if s > 4 and s % 4 == 0:
                        spread_den(b, s // 4 - 2)
                    if s == 3 and not has_last:
                        store_ip_values(tn)
                    if s == 5 and not has_last:
                        lay_blocks()
                    if s == 4 and has_next:
                        store_parts(0, b + 1)
                        store_parts(1, b + 1)
                    if s == 17 and has_last:
                        for i in range(NT - 1):
                            store_output(b - 1, i, tn)
                    if s == 8 and has_next:
                        fill_stacks(0, b + 1, UNITS * b + 32)
                        for i in range(2, NP):
                            store_parts(i, b + 1)
                    if s == 8 and has_next and not (isinstance(b, int) and b == B - 2):
                        sp.wait_ge(work_done, tn.done(("qk", 2)))
                        load_x(b + 2)
                    if s % 4 == 2 and s > 4:
                        place_output(b, s // 4 - 1, tn)
                    if s == 16 and has_next:
                        fill_stacks(1, b + 1, UNITS * b + 64)
                        if not (isinstance(b, int) and b == B - 2):
                            sp.wait_ge(work_done, tn.done(("v", NT - 1)))
                            load_ctx(b + 2)
                    if s == STEPS - 1:
                        spread_den(b, NG - 2)
                if has_last:
                    store_output(b - 1, NT - 1, tn)
                load_residual(b)

            sp.dma_start(wq[:, 0:2, :], w_q[0:256].rearrange("(t p) d -> p t d", p=128)).then_inc(wq_in, 16)
            sp.dma_start(wq[0:TILES[-1][1], ND - 1, :], w_q[256:D]).then_inc(wq_in, 16)
            load_x(0)
            load_ctx(0)
            sp.dma_start(cipT[:, :, :], ctx_ip_t.rearrange("(c p) m -> p c m", p=128)).then_inc(cip_in, 16)
            sp.dma_start(idf[:, :], eye).then_inc(eye_in, 16)
            store_parts(0, 0)
            fill_stack(0, 0, 0, None, range(2))
            store_parts(1, 0)
            fill_stack(0, 0, 0, None, range(2, len(PAIRS)))
            fill_stack(1, 0, 0, None)
            for i in range(2, NP):
                store_parts(i, 0)
            fill_stacks(1, 0, None)
            put_maxima(0, PRO)
            sp.wait_ge(m_rows, 16)
            load_x(1)
            load_ctx(1)
            fill_stacks(2, 0, None)
            stack_ip_keys()
            for t, rows in TILES:
                sp.dma_start(wo[0:rows, t, :], w_out[128 * t:128 * t + rows]).then_inc(wo_in, 16)
            sp.dma_start(bias[:, :], b_out.unsqueeze(0).broadcast_to([128, D])).then_inc(bias_in, 16)

            iteration(0, False, True)
            for b in range(1, B - 1):
                iteration(b, True, True)
            iteration(B - 1, True, False)
            place_output(B - 1, NG - 1)
            spread_den(B - 1, NG - 1)
            for i in range(NT):
                store_output(B - 1, i, EPI)
            sp.wait_ge(stored, 16 * NT * B)
            for t in range(ND):
                sp.wait_ge(stacked[t], 16 * 2 * len(PAIRS) * B)

        @block.tensor
        def _(pe):
            def taken(task, tn):
                pe.wait_ge(work_free[tn.bank(task)], tn.uses(task) + 1)

            def task(which, b, tn):
                kind, i = which
                bank = work[tn.bank(which)]
                uses = tn.uses(which)
                if not (isinstance(uses, int) and uses == 0):
                    pe.wait_ge(work_free[tn.bank(which)], uses)
                if kind == "q":
                    if i == 0:
                        pe.wait_ge(x_in, 16 * ND * (b + 1))
                    for c in range(ND):
                        last = nc.tensor.matmul(bank[:, :], wq[:, c, 128 * i:128 * (i + 1)],
                                                xT[:, c, :], start=(c == 0), stop=(c == ND - 1))
                elif kind == "k":
                    if i == 0:
                        pe.wait_ge(c_in, 16 * (b + 1))
                    for c in range(NC):
                        last = nc.tensor.matmul(bank[:, :], wk[:, c, 128 * i:128 * (i + 1)],
                                                cT[:, c, :], start=(c == 0), stop=(c == NC - 1))
                elif kind == "qk":
                    for c in range(NC):
                        if c < ND:
                            nc.tensor.matmul(bank[0:64, :], wq[:, c, 128 * i:D], xT[:, c, :],
                                             start=(c == 0), stop=(c == ND - 1))
                        last = nc.tensor.matmul(bank[64:128, :], wk[:, c, 128 * i:D], cT[:, c, :],
                                                start=(c == 0), stop=(c == NC - 1))
                elif kind == "v":
                    for c in range(NC):
                        if tn is PRO:
                            mx(0, i, c)
                        last = nc.tensor.matmul(bank[0:KT, 0:D], cT[:, c, i * KT:(i + 1) * KT], wv[:, c, :],
                                                start=(c == 0), stop=(c == NC - 1))
                elif kind == "mt":
                    pe.wait_ge(m_parts, NG * b + i + 1)
                    last = nc.tensor.transpose(bank[:, :].bitcast(bf16)[0:3 * GH * NT, 0:128], mparts[:, :], idb[:, :])
                elif kind in ("ips", "ips_first"):
                    if kind == "ips_first":
                        pe.wait_ge(kip_in, 16 * len(PAIRS))
                    for n in range(NT):
                        for j in range(GH):
                            h = i * GH + j
                            last = nc.tensor.matmul(bank[:, (n * GH + j) * NIP:(n * GH + j + 1) * NIP],
                                                    qst[0:SR, h, n * QT:(n + 1) * QT],
                                                    kipst[:, h, NIP * b:NIP * b + NIP],
                                                    start=True, stop=True)
                elif kind == "pt":
                    pe.wait_ge(ip_probs, b + 1)
                    cols = min(128, H * NIP - 128 * i)
                    for n in range(NT):
                        last = nc.tensor.transpose(bank[0:cols, n * QT:(n + 1) * QT],
                                                   ipp[:, n, 128 * i:128 * i + cols], idf[:, :])
                elif kind == "oip":
                    if i == 0:
                        taken(("pt", 0), tn)
                        taken(("pt", 1), tn)
                        pe.wait_ge(vb_made, b + 1)
                    last = nc.tensor.matmul(bank[0:TILES[i][1], :], vb[:, i, 0:TILES[i][1]], pT[:, i // 2, :],
                                            start=True, stop=True)
                elif kind == "f":
                    if i == 0:
                        pe.wait_ge(wo_in, 16 * ND)
                        for t in range(ND):
                            taken(("oip", t), tn)
                    for t in range(ND):
                        last = nc.tensor.matmul(bank[:, 0:D], oT[:, t, i * QT:(i + 1) * QT], wo[:, t, :],
                                                start=(t == 0), stop=(t == ND - 1))
                elif kind == "kip":
                    pe.wait_ge(cip_in, 16)
                    pe.wait_ge(wip_in, 16)
                    for t, rows in TILES:
                        for c in range(NC):
                            last = nc.tensor.matmul(bank[0:rows, t * B * NIP:(t + 1) * B * NIP],
                                                    wip[:, c, 128 * t:128 * t + rows], cipT[:, c, :],
                                                    start=(c == 0), stop=(c == NC - 1))
                elif kind == "vip":
                    pe.wait_ge(wip_in, 32)
                    for c in range(NC):
                        last = nc.tensor.matmul(bank[0:B * NIP, 0:D], cipT[:, c, :], wip[:, c, :],
                                                start=(c == 0), stop=(c == NC - 1))
                last.then_inc(work_done, 1)

            def st(b, s, j):
                g, kt = s // NT, s % NT
                h = g * GH + j
                i = UNITS * b + s * SLOTS + j
                if kt == 0 and j == 0:
                    pe.wait_ge(m_rows, 16 * (NG * b + g + 1))
                if not (isinstance(i, int) and i < 2):
                    pe.wait_ge(exp_done, i - 1)
                nc.tensor.matmul(st_bank[j % 2][0:KT, :], kst[:, h, kt * KT:(kt + 1) * KT], qst[:, h, :],
                                 start=True, stop=True).then_inc(st_done, 1)

            def mx(b, u, j):
                g, n = u // NT, u % NT
                h = g * GH + j
                i = UNITS * b + u * SLOTS + j
                if n == 0 and j == 0 and g % 2 == 0:
                    pe.wait_ge(stacked[g // 2], 16 * 2 * len(PAIRS) * (b + 1))
                if not (isinstance(i, int) and i < 2):
                    pe.wait_ge(mx_read, i - 1)
                nc.tensor.matmul(mx_bank[j % 2][:, 0:T], qst[0:SR, h, n * QT:(n + 1) * QT], kst[0:SR, h, :],
                                 start=True, stop=True).then_inc(mx_done, 1)

            def pv(b, s):
                g, kt = s // NT, s % NT
                if kt == 0:
                    pe.wait_ge(values_made, NG * b + g + 1)
                    earlier = NG * b + g - {0: 1, 1: 3}.get(g, 2)
                    if not (isinstance(earlier, int) and earlier < 0):
                        pe.wait_ge(og_made, earlier + 1)
                pe.wait_ge(exp_done, UNITS * b + (s + 1) * SLOTS)
                for j in range(GH):
                    last = nc.tensor.matmul(pv_bank[g % 2][32 * j:32 * (j + 1), :], vaug[:, kt, g * GH + j, :],
                                            P[:, s % 2, j, :], start=(kt == 0), stop=(kt == NT - 1))
                last.then_inc(pv_done, 1)

            def iteration(b, has_last, has_next):
                tn = turns(b, has_last, has_next)
                tasks = plan(has_last, has_next)
                for s in range(STEPS):
                    for j in range(SLOTS):
                        st(b, s, j)
                        u = s + LEAD
                        if u < STEPS:
                            mx(b, u, j)
                        elif has_next:
                            mx(b + 1, u - STEPS, j)
                        if (s, j) in tasks:
                            which = tasks[s, j]
                            task(which, batch_of(which, b), tn)
                        if j == 1 and s > 0:
                            pv(b, s - 1)
                pv(b, STEPS - 1)

            pe.wait_ge(zeroed_v, 4)
            pe.wait_ge(wq_in, 32)
            for which in PROLOGUE:
                if which == ("k", 0):
                    pe.wait_ge(wk_in, 16)
                if which == ("v", 0):
                    pe.wait_ge(wv_in, 16)
                if which == ("mt", 0):
                    pe.wait_ge(idb_made, 1)
                task(which, 0, PRO)
            for u in range(NT, LEAD):
                for j in range(SLOTS):
                    mx(0, u, j)
            iteration(0, False, True)
            for b in range(1, B - 1):
                iteration(b, True, True)
            iteration(B - 1, True, False)
            for which in EPILOGUE:
                task(which, B - 1, EPI)

        @block.scalar
        def _(act):
            def copy_out(dst, src, which, tn):
                nc.scalar.activation(dst, src, ACT.Copy).then_inc(work_free[tn.bank(which)], 1)

            def task(which, b, tn):
                kind, i = which
                if kind in ("oip", "f"):
                    return
                bank = work[tn.bank(which)]
                act.wait_ge(work_done, tn.done(which))
                if which in PROJ:
                    n = PROJ.index(which)
                    if not (isinstance(b, int) and b == 0):
                        act.wait_ge(parts_out[n], 16 * b)
                    nc.scalar.activation(parts[:, n, 0, :], bank[:, :], ACT.Copy).then_inc(first_part, 1)
                elif kind == "v":
                    if i == 0 and not (isinstance(b, int) and b == 0):
                        act.wait_ge(values_made, NG * b)
                    copy_out(vst[:, i, :], bank[0:KT, 0:D], which, tn)
                elif kind == "mt":
                    n = NG * b + i
                    if not (isinstance(n, int) and n == 0):
                        act.wait_ge(m_rows, 16 * n)
                    copy_out(mT[:, :], bank[:, :].bitcast(bf16)[0:3 * GH * NT, 0:128], which, tn)
                elif kind in ("ips", "ips_first"):
                    if not (isinstance(b, int) and b == 0):
                        act.wait_ge(ip_masked, b)
                    nc.scalar.activation(ips[:, :, i * GH * NIP:(i + 1) * GH * NIP],
                                         bank[:, 0:NT * GH * NIP].rearrange("p (n c) -> p n c", n=NT),
                                         ACT.Copy, scale=SCALE).then_inc(work_free[tn.bank(which)], 1)
                elif kind == "pt":
                    cols = min(128, H * NIP - 128 * i)
                    copy_out(pT[0:cols, i, :], bank[0:cols, :], which, tn)
                elif kind == "kip":
                    for t, rows in TILES:
                        nc.scalar.activation(kipp[0:rows, 0, t], bank[0:rows, t * B * NIP:(t + 1) * B * NIP],
                                             ACT.Copy).then_inc(kip_first, 1)
                elif kind == "vip":
                    copy_out(vips[:, :], bank[0:B * NIP, 0:D], which, tn)

            def exp(b, s, j):
                i = UNITS * b + s * SLOTS + j
                act.wait_ge(st_done, i + 1)
                step = STEPS * b + s
                if j == 0 and not (isinstance(step, int) and step < 2):
                    act.wait_ge(pv_done, step - 1)
                nc.scalar.activation(P[:, s % 2, j, :], st_bank[j % 2][0:KT, :], ACT.Exp,
                                     scale=SCALE).then_inc(exp_done, 1)

            def take_output(b, g):
                n = NG * b + g
                act.wait_ge(pv_done, NT * (n + 1))
                earlier = n - {0: 1, 1: 3}.get(g, 2)
                if not (isinstance(earlier, int) and earlier < 0):
                    act.wait_ge(og_out, 16 * (earlier + 1))
                nc.scalar.activation(og[:, g % 2, :], pv_bank[g % 2][:, :], ACT.Copy).then_inc(og_made, 1)

            def iteration(b, has_last, has_next):
                tn = turns(b, has_last, has_next)
                tasks = plan(has_last, has_next)
                for s in range(STEPS):
                    for j in range(SLOTS):
                        exp(b, s, j)
                        if (s, j) in tasks:
                            which = tasks[s, j]
                            task(which, batch_of(which, b), tn)
                        if j == 2 and s > 0 and s % NT == 0:
                            take_output(b, s // NT - 1)
                        if (s, j) == (17, 0):
                            act.wait_ge(ip_shifted, b + 1)
                            nc.scalar.activation(ipp[:, :, :], ipp[:, :, :], ACT.Exp).then_inc(ip_exp, 1)
                take_output(b, NG - 1)

            act.dma_start(wk[:, :, :], w_k.rearrange("(c p) d -> p c d", p=128)).then_inc(wk_in, 16)
            act.dma_start(boxes[:, :, :, :].rearrange("p b m c -> p (b m c)"),
                          bbox.rearrange("b m c -> (b m c)").unsqueeze(0).broadcast_to([128, B * 16])).then_inc(box_in, 16)
            act.dma_start(gxy[:, :, :], grid.rearrange("(n p) c -> p n c", p=QT)).then_inc(box_in, 16)
            act.wait_ge(c_in, 16)
            act.dma_start(wip[:, :, :], w_k_ip.rearrange("(c p) d -> p c d", p=128)).then_inc(wip_in, 16)
            act.dma_start(wv[:, :, :], w_v.rearrange("(c p) d -> p c d", p=128)).then_inc(wv_in, 16)
            for which in PROLOGUE:
                task(which, 0, PRO)
                if which == ("v", 0):
                    act.dma_start(wip[:, :, :], w_v_ip.rearrange("(c p) d -> p c d", p=128)).then_inc(wip_in, 16)
            iteration(0, False, True)
            for b in range(1, B - 1):
                iteration(b, True, True)
            iteration(B - 1, True, False)
            for which in EPILOGUE:
                task(which, B - 1, EPI)

        @block.vector
        def _(dve):
            def task(which, b, tn):
                kind, i = which
                if kind not in ("q", "k", "qk", "oip", "f", "kip"):
                    return
                bank = work[tn.bank(which)]
                free = work_free[tn.bank(which)]
                if which in PROJ:
                    p = PROJ.index(which)
                    n = NP * b + p
                    dve.wait_ge(first_part, n + 1)
                    if not (isinstance(n, int) and n < 2):
                        dve.wait_ge(parts_made, n if p == 0 else n - 1)
                    nc.vector.tensor_tensor(resid[:, p % 2, :], bank[:, :], parts[:, p, 0, :],
                                            ALU.subtract).then_inc(free, 1)
                    dve.wait_ge(free, tn.uses(which) + 1)
                    nc.vector.tensor_copy(parts[:, p, 1, :], resid[:, p % 2, :]).then_inc(second_part, 1)
                elif kind == "oip":
                    rows = TILES[i][1]
                    dve.wait_ge(work_done, tn.done(which))
                    dve.wait_ge(normed, ND * b + i + 1)
                    nc.vector.tensor_tensor(oT[0:rows, i, :], bank[0:rows, :], num[0:rows, i, :],
                                            ALU.add).then_inc(free, 1)
                elif kind == "f":
                    dve.wait_ge(work_done, tn.done(which))
                    if i == 0:
                        dve.wait_ge(res_made, b + 1)
                        if not (isinstance(b, int) and b == 0):
                            dve.wait_ge(stored, 16 * NT * b)
                    nc.vector.tensor_tensor(ob[:, i, :], bank[:, 0:D], xres[:, i, :], ALU.add).then_inc(free, 1)
                elif kind == "kip":
                    w = B * NIP
                    dve.wait_ge(kip_first, ND)
                    for t, rows in TILES:
                        nc.vector.tensor_tensor(kipr[0:rows, t], bank[0:rows, t * w:(t + 1) * w],
                                                kipp[0:rows, 0, t], ALU.subtract).then_inc(kip_step, 1)
                    dve.wait_ge(kip_step, ND)
                    for t, rows in TILES:
                        nc.vector.tensor_copy(kipp[0:rows, 1, t], kipr[0:rows, t]).then_inc(kip_step, 1)
                    dve.wait_ge(kip_step, 2 * ND)
                    for t, rows in TILES:
                        last = nc.vector.tensor_tensor(kipp[0:rows, 2, t], kipr[0:rows, t], kipp[0:rows, 1, t], ALU.subtract)
                        if t < ND - 1:
                            last.then_inc(kip_step, 1)
                    last.then_inc(kip_parts, 1)
                    dve.wait_ge(kip_parts, 1)
                    nc.vector.memset(kipr[0:1, 0, 0:1], 0.0).then_inc(free, 1)

            def row_max(b, u, j):
                n = u % NT
                i = UNITS * b + u * SLOTS + j
                dve.wait_ge(mx_done, i + 1)
                nc.vector.tensor_reduce(mrow[:, j * NT + n:j * NT + n + 1], mx_bank[j % 2][:, 0:T],
                                        axis=AX.X, op=ALU.max).then_inc(mx_read, 1)

            def cut_maxima(b, g):
                n = NG * b + g
                w = GH * NT
                dve.wait_ge(mx_read, UNITS * b + (g + 1) * NT * SLOTS)
                nc.vector.tensor_scalar(mparts[:, 0:w], mrow[:, :], -1.0, None, ALU.mult).then_inc(m_step, 1)
                dve.wait_ge(m_step, 3 * n + 1)
                nc.vector.scalar_tensor_tensor(out=mres[:, :], in0=mrow[:, :], scalar=-1.0, in1=mparts[:, 0:w],
                                               op0=ALU.mult, op1=ALU.subtract).then_inc(m_step, 1)
                dve.wait_ge(m_step, 3 * n + 2)
                nc.vector.tensor_copy(mparts[:, w:2 * w], mres[:, :]).then_inc(m_step, 1)
                dve.wait_ge(m_step, 3 * n + 3)
                nc.vector.tensor_tensor(mparts[:, 2 * w:3 * w], mres[:, :], mparts[:, w:2 * w],
                                        ALU.subtract).then_inc(m_parts, 1)

            def invert_den(b, g):
                dve.wait_ge(den_in, 16 * (NG * b + g + 1))
                nc.vector.reciprocal(denc[:, g % 2, :], denc[:, g % 2, :]).then_inc(den_inv, 1)

            def iteration(b, has_last, has_next):
                tn = turns(b, has_last, has_next)
                tasks = plan(has_last, has_next)
                for s in range(STEPS):
                    for j in range(SLOTS):
                        u = s + LEAD
                        if u < STEPS:
                            row_max(b, u, j)
                        elif has_next:
                            row_max(b + 1, u - STEPS, j)
                        if j == SLOTS - 1 and s % NT == 1:
                            if u < STEPS:
                                cut_maxima(b, u // NT)
                            elif has_next:
                                cut_maxima(b + 1, u // NT - NG)
                        if (s, j) in tasks:
                            which = tasks[s, j]
                            task(which, batch_of(which, b), tn)
                        if (s, j) == (2, 2) and has_last:
                            invert_den(b - 1, NG - 1)
                        if s > 4 and (s % NT, j) == (3, 2):
                            invert_den(b, s // NT - 1)
                        if (s, j) == (16, 0):
                            dve.wait_ge(ip_masked, b + 1)
                            nc.vector.tensor_reduce(ipmax[:, :], ipp[:, :, :].rearrange("p n (h k) -> p (n h) k", k=NIP),
                                                    axis=AX.X, op=ALU.max).then_inc(ip_max, 1)
                        if (s, j) == (18, 0):
                            dve.wait_ge(ip_exp, b + 1)
                            nc.vector.tensor_reduce(ipden[:, :], ipp[:, :, :].rearrange("p n (h k) -> p (n h) k", k=NIP),
                                                    axis=AX.X, op=ALU.add).then_inc(ip_step, 1)
                            dve.wait_ge(ip_step, b + 1)
                            nc.vector.reciprocal(ipden[:, :], ipden[:, :]).then_inc(ip_inv, 1)

            for padded in (xT, wq, wo, oT):
                nc.vector.memset(padded[TILES[-1][1]:128, ND - 1, :], 0.0).then_inc(zeroed_v, 1)
            dve.wait_ge(box_in, 32)
            for e, (corner, axis, op) in enumerate(((0, 0, ALU.is_ge), (1, 1, ALU.is_ge), (2, 0, ALU.is_le), (3, 1, ALU.is_le))):
                for b in range(B):
                    nc.vector.tensor_tensor(
                        cmp[:, e, 16 * b:16 * (b + 1)].rearrange("p (n m) -> p n m", n=NT),
                        gxy[:, :, axis:axis + 1].broadcast_to([128, NT, 4]),
                        boxes[:, b, :, corner].unsqueeze(1).broadcast_to([128, NT, 4]), op).then_inc(box_step, 1)
            dve.wait_ge(box_step, 4 * B)
            nc.vector.tensor_tensor(cmp[:, 0], cmp[:, 0], cmp[:, 1], ALU.mult).then_inc(box_step, 1)
            nc.vector.tensor_tensor(cmp[:, 2], cmp[:, 2], cmp[:, 3], ALU.mult).then_inc(box_step, 1)
            dve.wait_ge(box_step, 4 * B + 2)
            nc.vector.tensor_tensor(cmp[:, 0], cmp[:, 0], cmp[:, 2], ALU.mult).then_inc(box_step, 1)
            dve.wait_ge(box_step, 4 * B + 3)
            inside = cmp[:, 0].rearrange("p (n m) -> p n m", m=4)
            nc.vector.tensor_reduce(anyin[:, :], inside, axis=AX.X, op=ALU.max).then_inc(box_step, 1)
            mask_rows = mask[:, :, :, :].rearrange("p b n k -> p (b n) k")
            nc.vector.tensor_scalar(mask_rows[:, :, 4:8], inside, 1.0, -NEG, ALU.subtract, ALU.mult).then_inc(mask_made, 1)
            dve.wait_ge(box_step, 4 * B + 4)
            nc.vector.tensor_scalar(mask_rows[:, :, 0:4], anyin[:, :].unsqueeze(2).broadcast_to([128, B * NT, 4]),
                                    NEG, None, ALU.mult).then_inc(mask_made, 1)
            for which in PROLOGUE:
                if which == ("v", 0):
                    dve.wait_ge(eye_in, 16)
                    nc.vector.tensor_copy(idb[:, :], idf[:, :]).then_inc(idb_made, 1)
                if which[0] == "v":
                    for j in range(SLOTS):
                        row_max(0, which[1], j)
                if which == ("mt", 0):
                    cut_maxima(0, 0)
                task(which, 0, PRO)
            for u in range(NT, LEAD):
                for j in range(SLOTS):
                    row_max(0, u, j)
            iteration(0, False, True)
            for b in range(1, B - 1):
                iteration(b, True, True)
            iteration(B - 1, True, False)
            invert_den(B - 1, NG - 1)
            for which in EPILOGUE:
                task(which, B - 1, EPI)

        @block.gpsimd
        def _(pool):
            def cut(p, b, tn):
                n = NP * b + p
                pool.wait_ge(second_part, n + 1)
                if not (isinstance(b, int) and b == 0):
                    pool.wait_ge(parts_out[p], 16 * b)
                nc.gpsimd.tensor_tensor(out=parts[:, p, 2, :], in0=resid[:, p % 2, :], in1=parts[:, p, 1, :],
                                        op=ALU.subtract).then_inc(parts_made, 1)

            def lay_values(b, g, tn):
                if g == 0:
                    for i in (NT - 2, NT - 1):
                        pool.wait_ge(work_free[tn.bank(("v", i))], tn.uses(("v", i)) + 1)
                if not (isinstance(b, int) and b == 0):
                    pool.wait_ge(pv_done, STEPS * (b - 1) + NT * (g + 1))
                nc.gpsimd.tensor_copy(
                    vaug[:, :, g * GH:(g + 1) * GH, 0:DH],
                    vst[:, :, g * GH * DH:(g + 1) * GH * DH].rearrange("p n (h d) -> p n h d", d=DH)).then_inc(values_made, 1)

            def normalise(b, t):
                rows = TILES[t][1]
                pool.wait_ge(placed[t], (b + 1) * (64 if t < 2 else 32))
                nc.gpsimd.tensor_tensor(out=num[0:rows, t], in0=num[0:rows, t], in1=den[0:rows, t],
                                        op=ALU.mult).then_inc(normed, 1)

            def add_bias(b):
                pool.wait_ge(xres_in, 16 * (b + 1))
                nc.gpsimd.tensor_tensor(out=xres[:, :, :], in0=xres[:, :, :],
                                        in1=bias[:, :].unsqueeze(1).broadcast_to([128, NT, D]),
                                        op=ALU.add).then_inc(res_made, 1)

            heads = ipp[:, :, :].rearrange("p n (h k) -> p (n h) k", k=NIP)

            def mask_scores(b, tn):
                pool.wait_ge(work_free[tn.bank(("ips", 4))], tn.uses(("ips", 4)) + 1)
                if tn.has(("pt", 1)):
                    pool.wait_ge(work_done, tn.done(("pt", 1)))
                for n in range(NT):
                    last = nc.gpsimd.tensor_tensor(
                        out=ipp[:, n].rearrange("p (h k) -> p h k", k=NIP),
                        in0=ips[:, n].rearrange("p (h k) -> p h k", k=NIP),
                        in1=mask[:, b, n, :].unsqueeze(1).broadcast_to([128, H, NIP]), op=ALU.add)
                last.then_inc(ip_masked, 1)

            def shift(b):
                pool.wait_ge(ip_max, b + 1)
                nc.gpsimd.tensor_tensor(out=heads, in0=heads, in1=ipmax[:, :].unsqueeze(2).broadcast_to([128, NT * H, NIP]),
                                        op=ALU.subtract).then_inc(ip_shifted, 1)

            def probabilities(b):
                pool.wait_ge(ip_inv, b + 1)
                nc.gpsimd.tensor_tensor(out=heads, in0=heads, in1=ipden[:, :].unsqueeze(2).broadcast_to([128, NT * H, NIP]),
                                        op=ALU.mult).then_inc(ip_probs, 1)

            def lay_ip_values(b, tn):
                if isinstance(b, int) and b == 0:
                    pool.wait_ge(vblocks_in, 16 * H)
                if tn.has(("oip", 2)):
                    pool.wait_ge(work_done, tn.done(("oip", 2)))
                nc.gpsimd.tensor_copy(vb[:, :, :], vblocks[:, b, :, :]).then_inc(vb_made, 1)

            def iteration(b, has_last, has_next):
                tn = turns(b, has_last, has_next)
                if has_last:
                    lay_values(b, NG - 1, None)
                    if not has_next:
                        normalise(b - 1, 2)
                        add_bias(b - 1)
                if has_next:
                    for p in range(NP):
                        cut(p, b + 1, tn)
                        if p == 1 and has_last:
                            normalise(b - 1, 2)
                        if p == 2 and has_last:
                            add_bias(b - 1)
                normalise(b, 0)
                lay_ip_values(b, tn)
                mask_scores(b, tn)
                if has_next:
                    for g in range(3):
                        lay_values(b + 1, g, tn)
                shift(b)
                if has_next:
                    lay_values(b + 1, 3, tn)
                probabilities(b)
                normalise(b, 1)


            pair_of_ones = 1.0 + 0x3F80 / 2.0 ** 23
            nc.gpsimd.memset(qst[96:128, :, :].rearrange("p h s -> p (h s)").bitcast(fp32), 0.0).then_inc(zeroed_p, 1)
            nc.gpsimd.memset(kst[96:128, :, :].rearrange("p h s -> p (h s)").bitcast(fp32), pair_of_ones).then_inc(zeroed_p, 1)
            pool.wait_ge(zeroed_p, 2)
            nc.gpsimd.memset(vblocks[:, :, :, :].rearrange("p b t c -> p (b t c)"), 0.0).then_inc(zeroed_p, 1)
            pool.wait_ge(zeroed_p, 3)
            nc.gpsimd.memset(pT[:, 1, :], 0.0).then_inc(zeroed_p, 1)
            pool.wait_ge(zeroed_p, 4)
            nc.gpsimd.memset(vaug[:, :, :, :].rearrange("p n h c -> p (n h c)"), 1.0).then_inc(zeroed_p, 1)
            pool.wait_ge(zeroed_p, 5)
            for p in range(NP):
                cut(p, 0, PRO)
            for g in range(NG):
                lay_values(0, g, PRO)
            pool.wait_ge(bias_in, 16)
            pool.wait_ge(mask_made, 2)
            iteration(0, False, True)
            for b in range(1, B - 1):
                iteration(b, True, True)
            iteration(B - 1, True, False)
            add_bias(B - 1)
            normalise(B - 1, 2)


_INS = ['fside_Bx4x4_0', 'L0_xattn_w_q', 'L0_xattn_w_k', 'L0_xattn_w_v',
        'L0_xattn_w_k_ip', 'L0_xattn_w_v_ip', 'L0_xattn_w_out', 'L0_xattn_b_out']


def kernel(**inputs):
    import numpy as _np
    import concourse.bacc as _bacc
    from concourse import mybir as _mybir
    from concourse.bass_utils import run_bass_kernel_spmd as _run

    nc = _bacc.Bacc("TRN2", target_bir_lowering=False, num_devices=1)
    arrays, args = {}, []

    def give(name, a):
        arrays[name] = a
        args.append(nc.dram_tensor(name, a.shape, _mybir.dt.from_np(a.dtype), kind="ExternalInput").ap())

    text = inputs['ctx_2048'].shape[1] - 8
    give("in_x_dram", _np.ascontiguousarray(inputs['x']))
    give("in_x_t_dram", _np.ascontiguousarray(_np.transpose(inputs['x'], (0, 2, 1))))
    give("in_ctx_t_dram", _np.ascontiguousarray(_np.transpose(inputs['ctx_2048'], (0, 2, 1))))
    give("in_ctx_ip_t_dram", _np.ascontiguousarray(
        _np.transpose(inputs['ctx_2048'][:, text:], (2, 0, 1))).reshape(inputs['ctx_2048'].shape[2], -1))
    for name in _INS:
        give(f"in_{name}_dram", _np.ascontiguousarray(inputs[name]))
    seq = inputs['x'].shape[1]
    width = next(w for w in range(int(seq ** 0.5), seq + 1) if seq % w == 0)

    def line(n):
        c = _np.arange(n, dtype=_np.float32) * (_np.float32(1) / _np.float32(n - 1))
        c[-1] = 1
        return c
    pos = _np.arange(seq)
    grid = _np.stack([line(width)[pos % width], line(seq // width)[pos // width]], axis=1)
    give("grid_dram", _np.ascontiguousarray(grid))
    give("eye_dram", _np.eye(128, dtype=_np.float32))
    shape = tuple(inputs['x'].shape)
    args.append(nc.dram_tensor("out_0_dram", shape, _mybir.dt.float32, kind="ExternalOutput").ap())
    cross_attention_kernel(nc, *args)
    r = _run(nc, [arrays], core_ids=[0])
    return r.results[0]["out_0_dram"]
```

```python
import concourse.bass as bass
from concourse import mybir
from contextlib import ExitStack


def cross_attention_kernel(
    nc: bass.Bass,
    x: bass.AP,
    x_t: bass.AP,
    ctx_t: bass.AP,
    ctx_ip_t: bass.AP,
    bbox: bass.AP,
    w_q: bass.AP,
    w_k: bass.AP,
    w_v: bass.AP,
    w_k_ip: bass.AP,
    w_v_ip: bass.AP,
    w_out: bass.AP,
    b_out: bass.AP,
    grid: bass.AP,
    eye: bass.AP,
    out: bass.AP,
):
    fp32 = mybir.dt.float32
    bf16 = mybir.dt.bfloat16
    ALU = mybir.AluOpType
    ACT = mybir.ActivationFunctionType
    AX = mybir.AxisListType

    B, S, D = x.shape
    C = ctx_t.shape[1]
    H, DH, NIP = 20, D // 20, 8
    T = ctx_t.shape[2] - NIP
    NEG = -10000.0
    GH = 4
    NG = H // GH
    NT = 4
    QT, KT = S // NT, T // NT
    HT = 128 // DH
    NC = C // 128
    TILES = [(t, min(128, D - 128 * t)) for t in range((D + 127) // 128)]
    ND = len(TILES)
    PAIRS = [(0, 0), (1, 0), (2, 0), (0, 1), (1, 1), (0, 2), (1, 2)]
    SR = DH * len(PAIRS)
    STEPS, SLOTS = NG * NT, GH
    UNITS = STEPS * SLOTS
    LEAD = 6
    WIDE = STEPS - LEAD + 1
    SCALE = float(DH) ** -0.5

    PLAN = {
        1: ("q", 0), 4: ("k", 0), 8: ("pt", 0), 10: ("mt", 1), 11: ("ips", 1), 12: ("pt", 1),
        13: ("q", 1), 16: ("k", 1), 21: ("oip", 0), 22: ("qk", 2), 26: ("mt", 2), 27: ("ips", 2),
        29: ("oip", 1), 34: ("oip", 2), 36: ("f", 0), 39: ("f", 1), 42: ("mt", 3), 43: ("ips", 3),
        44: ("v", 0), 48: ("v", 1), 52: ("v", 2), 58: ("mt", 4), 59: ("ips", 4), 60: ("v", 3),
        66: ("f", 2), 70: ("f", 3), 74: ("mt", 0), 75: ("ips", 0),
    }
    FIRST = {21: ("ips_first", 0), 36: ("vip", 0)}
    ENDING = {69: ("den", NG - 2), 70: ("num", NG - 2)}
    PIECES = {"q": ND, "k": NC, "qk": NC, "v": NC, "f": ND, "vip": NC}
    NEXT = ("q", "k", "qk", "v")
    LAST = ("pt", "oip", "f")
    BEFORE_MX = [("q", 0), ("k", 0), ("q", 1), ("k", 1), ("qk", 2), ("kip", 0)]
    PROLOGUE = BEFORE_MX + [("v", i) for i in range(NT - 1)] + [("mt", 0), ("v", NT - 1)]
    WARM_UP = 4
    EPILOGUE = [("pt", 0), ("pt", 1)] + [("oip", i) for i in range(ND)]
    PROJ = [("q", 0), ("k", 0), ("q", 1), ("k", 1), ("qk", 2)]
    NP = len(PROJ)

    def plan(has_last, has_next):
        def kept(task):
            if task[0] in NEXT or task in (("mt", 0), ("ips", 0)):
                return has_next
            return has_last or task[0] not in LAST
        kept_tasks = {at: task for at, task in PLAN.items() if kept(task)}
        if not has_last:
            kept_tasks.update(FIRST)
            kept_tasks[29] = kept_tasks.pop(11)
        if not has_next:
            kept_tasks[44] = kept_tasks.pop(66)
            kept_tasks[48] = kept_tasks.pop(70)
            kept_tasks[52] = kept_tasks.pop(59)
            kept_tasks.update(ENDING)
        return kept_tasks

    def by_piece(has_last, has_next):
        return {at + c: (task, c) for at, task in plan(has_last, has_next).items()
                for c in range(PIECES.get(task[0], 1))}

    def by_end(has_last, has_next):
        return {at + PIECES.get(task[0], 1) - 1: task for at, task in plan(has_last, has_next).items()}

    def batch_of(task, b):
        if task[0] in NEXT or task in (("mt", 0), ("ips", 0)):
            return b + 1
        return b - 1 if task[0] in LAST else b

    class Turns:

        def __init__(self, tasks, half, odd):
            self.place = {task: n for n, task in enumerate(tasks)}
            self.half, self.odd = half, odd

        def has(self, task):
            return task in self.place

        def bank(self, task):
            return (self.place[task] + self.odd) % 2

        def uses(self, task):
            return self.half + (self.place[task] + self.odd) // 2

        def done(self, task):
            return self.half * 2 + self.odd + self.place[task] + 1

    N0 = len(PROLOGUE)
    N1 = len(plan(False, True))
    NB = len(PLAN)
    assert NB % 2 == 0

    def turns(b, has_last, has_next):
        tasks = [plan(has_last, has_next)[at] for at in sorted(plan(has_last, has_next))]
        if not has_last:
            return Turns(tasks, N0 // 2, N0 % 2)
        return Turns(tasks, (N0 + N1) // 2 + (b - 1) * (NB // 2), (N0 + N1) % 2)

    PRO = Turns(PROLOGUE, 0, 0)
    before_end = N0 + N1 + (B - 2) * NB + len(plan(True, False))
    END = turns(B - 1, True, False)
    EPI = Turns(EPILOGUE, before_end // 2, before_end % 2)

    ctx = ExitStack()
    with ctx:
        def sb(name, shape, dt=fp32):
            return ctx.enter_context(nc.sbuf_tensor(name, shape, dt))

        def pb(name):
            return ctx.enter_context(nc.psum_tensor(name, [128, 512], fp32))

        def sem(name):
            return ctx.enter_context(nc.semaphore(name))

        wq = sb("wq", [128, ND, D])
        wk = sb("wk", [128, NC, D])
        wv = sb("wv", [128, NC, D])
        wo = sb("wo", [128, ND, D])
        bias = sb("bias", [128, D])
        idf = sb("idf", [128, 128])
        idb = sb("idb", [128, 128], bf16)
        pick = sb("pick", [128, 2, GH * DH])
        xT = sb("xT", [128, ND, S])
        cT = sb("cT", [128, NC, T + NIP])
        parts = sb("parts", [128, NP, 3, S], bf16)
        resid = sb("resid", [128, 2, S])
        qst = sb("qst", [128, H, S], bf16)
        kst = sb("kst", [128, H, T], bf16)
        vst = sb("vst", [KT, NT, D])
        vaug = sb("vaug", [KT, NT, H, 2 * DH])
        mrow = sb("mrow", [128, GH * NT])
        mres = sb("mres", [128, GH * NT])
        mparts = sb("mparts", [128, 3 * GH * NT], bf16)
        mT = sb("mT", [3 * GH * NT, 128], bf16)
        P = sb("P", [KT, 2, GH, S])
        og = sb("og", [128, 2, S])
        num = sb("num", [128, ND, S])
        den = sb("den", [128, ND, S])
        denc = sb("denc", [128, 2, GH * S // 128])
        oT = sb("oT", [128, ND, S])
        xres = sb("xres", [128, NT, D])
        ob = sb("ob", [128, NT, D])
        tail_inv = sb("tail_inv", [128, S])
        tail_num = sb("tail_num", [128, S])
        cipT = sb("cipT", [128, NC, B * NIP])
        kipr = sb("kipr", [128, ND, B * NIP])
        kipp = sb("kipp", [128, 3, ND, B * NIP], bf16)
        kipst = sb("kipst", [SR, H, B * NIP], bf16)
        vips = sb("vips", [B * NIP, D])
        vblocks = sb("vblocks", [128, B, ND, 128])
        vb = sb("vb", [128, ND, 128])
        ips = sb("ips", [128, NT, H * NIP])
        ipp = sb("ipp", [128, NT, H * NIP])
        ipmax = sb("ipmax", [128, NT * H])
        ipden = sb("ipden", [128, NT * H])
        pT = sb("pT", [128, 2, S])
        boxes = sb("boxes", [128, B, 4, 4])
        gxy = sb("gxy", [128, NT, 2])
        compared = sb("compared", [128, 4, B * NT * 4])
        anyin = sb("anyin", [128, B * NT])
        mask = sb("mask", [128, B, NT, NIP])

        parts_d = nc.dram_tensor("parts_scratch", [NP, 3, 128, S], bf16, kind="Internal").ap()
        kip_d = nc.dram_tensor("kip_scratch", [3, D, B * NIP], bf16, kind="Internal").ap()
        vip_d = nc.dram_tensor("vip_scratch", [B * NIP, D], fp32, kind="Internal").ap()
        den_d = nc.dram_tensor("den_scratch", [NG, GH, S], fp32, kind="Internal").ap()
        og_d = nc.dram_tensor("og_scratch", [NG, GH, 2, DH, S], fp32, kind="Internal").ap()

        st_bank = [pb(f"st_bank{i}") for i in range(2)]
        mx_bank = [pb(f"mx_bank{i}") for i in range(2)]
        pv_bank = [pb(f"pv_bank{i}") for i in range(2)]
        work = [pb(f"work{i}") for i in range(2)]
        wide_bank = st_bank + mx_bank
        tail_bank = mx_bank + st_bank

        x_in, c_in, xres_in = sem("x_in"), sem("c_in"), sem("xres_in")
        wq_in, wk_in, wv_in, wo_in = sem("wq_in"), sem("wk_in"), sem("wv_in"), sem("wo_in")
        wip_in, eye_in, box_in, cip_in, bias_in = (sem("wip_in"), sem("eye_in"), sem("box_in"),
                                                   sem("cip_in"), sem("bias_in"))
        zeroed_v, zeroed_p, idb_made = sem("zeroed_v"), sem("zeroed_p"), sem("idb_made")
        work_done = sem("work_done")
        work_free = [sem(f"work_free{i}") for i in range(2)]
        first_part = sem("first_part")
        parts_made = sem("parts_made")
        second_part = sem("second_part")
        parts_out = [sem(f"parts_out{i}") for i in range(NP)]
        stacked = [sem(f"stacked{t}") for t in range(ND)]
        values_made = sem("values_made")
        mx_done, mx_read = sem("mx_done"), sem("mx_read")
        m_step, m_parts = sem("m_step"), sem("m_parts")
        m_rows = sem("m_rows")
        st_done, exp_done, pv_done = sem("st_done"), sem("exp_done"), sem("pv_done")
        og_made, og_out = sem("og_made"), sem("og_out")
        placed = [sem(f"placed{t}") for t in range(ND)]
        den_in = [sem("den_in_even"), sem("den_in_odd")]
        den_inv, den_out, normed = sem("den_inv"), sem("den_out"), sem("normed")
        kip_first, kip_step, kip_parts, kip_out, kip_in = (sem("kip_first"), sem("kip_step"),
                                                           sem("kip_parts"), sem("kip_out"), sem("kip_in"))
        vip_out, vblocks_in, vb_made = sem("vip_out"), sem("vblocks_in"), sem("vb_made")
        box_step, mask_made = sem("box_step"), sem("mask_made")
        ip_masked, ip_max, ip_shifted, ip_exp, ip_step, ip_inv, ip_probs = (
            sem("ip_masked"), sem("ip_max"), sem("ip_shifted"), sem("ip_exp"), sem("ip_step"),
            sem("ip_inv"), sem("ip_probs"))
        res_made, stored = sem("res_made"), sem("stored")
        pick_made = sem("pick_made")
        picked, tail_inverted, tail_normed, tail_made, tail_f, tail_ob = (
            sem("picked"), sem("tail_inverted"), sem("tail_normed"), sem("tail_made"),
            sem("tail_f"), sem("tail_ob"))

        wip = sb("wip", [128, NC, D])

        block = ctx.enter_context(nc.Block())

        @block.sync
        def _(sp):
            def ready(v):
                if not isinstance(v, int):
                    sp.lower_val(v)
                return v

            def after_next(b):
                if isinstance(b, int):
                    return b + 2
                return (b + 2 - b // (B - 2)).with_bounds(min_val=3, max_val=B - 1)

            def load_x(b):
                for t, rows in TILES:
                    sp.dma_start(xT[0:rows, t, :], x_t[b, 128 * t:128 * t + rows]).then_inc(x_in, 16)

            def load_ctx(b):
                sp.dma_start(cT[:, :, :], ctx_t[b].rearrange("(c p) n -> p c n", p=128)).then_inc(c_in, 16)

            def store_parts(i, b):
                cut, read = ready(NP * b + i + 1), ready(16 * 2 * len(PAIRS) * b)
                sp.wait_ge(parts_made, cut)
                if not (isinstance(b, int) and b == 0):
                    sp.wait_ge(stacked[i // 2], read)
                sp.dma_start(parts_d[i].rearrange("i r s -> r i s"), parts[:, i]).then_inc(parts_out[i], 16)

            def fill_stack(kind, t, b, units_done):
                rows = TILES[t][1]
                tile, r = (2 * t + kind, 0) if rows == 128 else (NP - 1, kind * rows)
                stack, width = (qst, S) if kind == 0 else (kst, T)
                stored_parts = ready(16 * (b + 1))
                if units_done is not None:
                    units_done = ready(units_done)
                sp.wait_ge(parts_out[tile], stored_parts)
                if units_done is None:
                    sp.wait_ge(zeroed_p, 2)
                else:
                    sp.wait_ge(st_done, units_done)
                for slot, pair in enumerate(PAIRS):
                    sp.dma_start(
                        stack[slot * DH:(slot + 1) * DH, t * HT:t * HT + rows // DH, :],
                        parts_d[tile, pair[kind], r:r + rows, 0:width].rearrange("(h d) s -> d h s", d=DH),
                    ).then_inc(stacked[t], 16)

            def fill_stacks(t, b, units_done):
                fill_stack(0, t, b, units_done)
                fill_stack(1, t, b, units_done)

            def put_maxima(g, tn):
                which = ("mt", g)
                sp.wait_ge(work_free[tn.bank(which)], tn.uses(which) + 1)
                sp.dma_start(qst[SR:SR + 3, g * GH:(g + 1) * GH, :].rearrange("i h s -> i (h s)"),
                             mT[:, :]).then_inc(m_rows, 16)

            def store_group(b, g):
                n = NG * b + g
                sp.wait_ge(og_made, n + 1)
                sp.dma_start(og_d[g].rearrange("j c d s -> (j c d) s"), og[:, g % 2]).then_inc(og_out, 16)

            def place_output(b, g, tn=None):
                n = NG * b + g
                t, r = g // 2, (g % 2) * GH * DH
                read = ("oip", t)
                over = g % 2 == 0 and tn is not None and tn.has(read)
                stored_group, uses = ready(16 * (n + 1)), ready(tn.uses(read) + 1) if over else None
                sp.wait_ge(og_out, stored_group)
                if over:
                    sp.wait_ge(work_free[tn.bank(read)], uses)
                sp.dma_start(denc[:, g % 2, :], og_d[g, :, 1, 0].rearrange("j (r w) -> j r w", r=128 // GH)).then_inc(den_in[g % 2], 16)
                sp.dma_start(num[r:r + GH * DH, t, :], og_d[g, :, 0]).then_inc(placed[t], 16)

            def spread_den(b, g):
                n = NG * b + g
                t, r = g // 2, (g % 2) * GH * DH
                sp.wait_ge(den_inv, n + 1)
                sp.dma_start(den_d[g].rearrange("j (r w) -> j r w", r=128 // GH), denc[:, g % 2, :]).then_inc(den_out, 16)
                sp.wait_ge(den_out, 16 * (n + 1))
                sp.dma_start(den[r:r + GH * DH, t, :],
                             den_d[g].unsqueeze(1).broadcast_to([GH, DH, S])).then_inc(placed[t], 16)

            def load_residual(b):
                if not (isinstance(b, int) and b == 0):
                    sp.wait_ge(stored, 16 * NT * b)
                sp.dma_start(xres[:, :, :], x[b].rearrange("(n p) d -> p n d", p=QT)).then_inc(xres_in, 16)

            def store_output(b, i, tn):
                sp.wait_ge(work_free[tn.bank(("f", i))], tn.uses(("f", i)) + 1)
                sp.dma_start(out[b, i * QT:(i + 1) * QT], ob[:, i]).then_inc(stored, 16)

            def stack_ip_keys():
                sp.wait_ge(kip_parts, 1)
                for t, rows in TILES:
                    sp.dma_start(kip_d[:, 128 * t:128 * t + rows].rearrange("i r m -> r i m"),
                                 kipp[0:rows, :, t]).then_inc(kip_out, 16)
                sp.wait_ge(kip_out, 16 * ND)
                for slot, pair in enumerate(PAIRS):
                    sp.dma_start(kipst[slot * DH:(slot + 1) * DH, :, :],
                                 kip_d[pair[1]].rearrange("(h d) m -> d h m", d=DH)).then_inc(kip_in, 16)

            def store_ip_values(tn):
                sp.wait_ge(work_free[tn.bank(("vip", 0))], tn.uses(("vip", 0)) + 1)
                sp.dma_start(vip_d, vips[:, :]).then_inc(vip_out, 16)

            def lay_blocks(heads):
                sp.wait_ge(vip_out, 16)
                sp.wait_ge(zeroed_p, 3)
                for h in heads:
                    t, r = h // HT, h % (2 * HT) * NIP
                    sp.dma_start(vblocks[r:r + NIP, :, t, h % HT * DH:(h % HT + 1) * DH],
                                 vip_d.rearrange("(b k) c -> k b c", k=NIP)[:, :, h * DH:(h + 1) * DH]).then_inc(vblocks_in, 16)

            def iteration(b, has_last, has_next):
                tn = turns(b, has_last, has_next)
                if has_last:
                    store_group(b - 1, NG - 1)
                    place_output(b - 1, NG - 1)
                if has_last and has_next:
                    spread_den(b - 1, NG - 2)
                put_maxima(1, tn)
                if not has_next:
                    spread_den(b - 1, NG - 2)
                if has_last:
                    spread_den(b - 1, NG - 1)
                    fill_stacks(2, b, UNITS * b)
                if has_next:
                    store_parts(0, b + 1)
                    store_parts(1, b + 1)
                put_maxima(2, tn)
                store_group(b, 0)
                place_output(b, 0, tn)
                if has_next:
                    fill_stacks(0, b + 1, UNITS * b + 8 * SLOTS)
                    for i in range(2, NP):
                        store_parts(i, b + 1)
                    sp.wait_ge(work_done, tn.done(("qk", 2)))
                    load_x(after_next(b))
                spread_den(b, 0)
                put_maxima(3, tn)
                if not has_last:
                    store_ip_values(tn)
                store_group(b, 1)
                place_output(b, 1, tn)
                if not has_last:
                    lay_blocks(range(0, 8))
                spread_den(b, 1)
                if has_next:
                    if not has_last:
                        lay_blocks(range(8, 12))
                    put_maxima(4, tn)
                    store_group(b, 2)
                    place_output(b, 2, tn)
                    if not has_last:
                        lay_blocks(range(12, 16))
                    fill_stack(0, 1, b + 1, UNITS * b + 16 * SLOTS)
                    spread_den(b, 2)
                    store_group(b, 3)
                    fill_stack(1, 1, b + 1, UNITS * b + 16 * SLOTS)
                    if has_last:
                        for i in range(NT - 1):
                            store_output(b - 1, i, tn)
                    put_maxima(0, tn)
                    place_output(b, 3, tn)
                    sp.wait_ge(work_done, tn.done(("v", NT - 1)))
                    load_ctx(after_next(b))
                    if has_last:
                        store_output(b - 1, NT - 1, tn)
                    if not has_last:
                        lay_blocks(range(16, 20))
                    load_residual(b)
                else:
                    for i in range(NT):
                        store_output(b - 1, i, tn)
                    store_group(b, 2)
                    put_maxima(4, tn)
                    load_residual(b)
                    place_output(b, 2, tn)
                    spread_den(b, 2)

            sp.dma_start(wq[:, 0:2, :], w_q[0:256].rearrange("(t p) d -> p t d", p=128)).then_inc(wq_in, 16)
            sp.dma_start(wq[0:TILES[-1][1], ND - 1, :], w_q[256:D]).then_inc(wq_in, 16)
            load_x(0)
            load_ctx(0)
            sp.dma_start(cipT[:, :, :], ctx_ip_t.rearrange("(c p) m -> p c m", p=128)).then_inc(cip_in, 16)
            sp.dma_start(idf[:, :], eye).then_inc(eye_in, 16)
            store_parts(0, 0)
            store_parts(1, 0)
            fill_stacks(0, 0, None)
            for i in range(2, NP):
                store_parts(i, 0)
            fill_stacks(1, 0, None)
            put_maxima(0, PRO)
            sp.wait_ge(m_rows, 16)
            load_x(1)
            sp.wait_ge(work_done, PRO.done(("v", NT - 1)))
            load_ctx(1)
            fill_stacks(2, 0, None)
            stack_ip_keys()
            for t, rows in TILES:
                sp.dma_start(wo[0:rows, t, :], w_out[128 * t:128 * t + rows]).then_inc(wo_in, 16)
            sp.dma_start(bias[:, :], b_out.unsqueeze(0).broadcast_to([128, D])).then_inc(bias_in, 16)

            iteration(0, False, True)
            with sp.Fori(1, B - 1) as b:
                iteration(b, True, True)
            iteration(B - 1, True, False)
            for i in range(NT):
                sp.wait_ge(tail_ob, i + 1)
                sp.dma_start(out[B - 1, i * QT:(i + 1) * QT], ob[:, i]).then_inc(stored, 16)
            sp.wait_ge(stored, 16 * NT * B)
            for t in range(ND):
                sp.wait_ge(stacked[t], 16 * 2 * len(PAIRS) * B)

        @block.tensor
        def _(pe):
            def taken(tasks, which, tn):
                other = [t for t in tasks if tn.bank(t) != tn.bank(which)]
                if other:
                    last = max(other, key=lambda t: tn.place[t])
                    pe.wait_ge(work_free[tn.bank(last)], tn.uses(last) + 1)

            def piece(which, c, b, tn):
                kind, i = which
                bank = work[tn.bank(which)]
                uses = tn.uses(which)
                ends = c == PIECES.get(kind, 1) - 1
                if c == 0 and not (isinstance(uses, int) and uses == 0):
                    pe.wait_ge(work_free[tn.bank(which)], uses)
                if kind == "q":
                    if i == 0 and c == 0:
                        pe.wait_ge(x_in, 16 * ND * (b + 1))
                    last = nc.tensor.matmul(bank[:, :], wq[:, c, 128 * i:128 * (i + 1)],
                                            xT[:, c, :], start=(c == 0), stop=ends)
                elif kind == "k":
                    if i == 0 and c == 0:
                        pe.wait_ge(c_in, 16 * (b + 1))
                    last = nc.tensor.matmul(bank[:, :], wk[:, c, 128 * i:128 * (i + 1)],
                                            cT[:, c, :], start=(c == 0), stop=ends)
                elif kind == "qk":
                    if c < ND:
                        nc.tensor.matmul(bank[0:64, :], wq[:, c, 128 * i:D], xT[:, c, :],
                                         start=(c == 0), stop=(c == ND - 1))
                    last = nc.tensor.matmul(bank[64:128, :], wk[:, c, 128 * i:D], cT[:, c, :],
                                            start=(c == 0), stop=ends)
                elif kind == "v":
                    last = nc.tensor.matmul(bank[0:KT, 0:D], cT[:, c, i * KT:(i + 1) * KT], wv[:, c, :],
                                            start=(c == 0), stop=ends)
                elif kind == "mt":
                    pe.wait_ge(m_parts, NG * b + i + 1)
                    last = nc.tensor.matmul(bank[0:3 * GH * NT, 0:128], mparts[:, :], idb[:, :], start=True, stop=True)
                elif kind in ("ips", "ips_first"):
                    if kind == "ips_first":
                        pe.wait_ge(kip_in, 16 * len(PAIRS))
                    for n in range(NT):
                        for j in range(GH):
                            h = i * GH + j
                            last = nc.tensor.matmul(bank[:, (n * GH + j) * NIP:(n * GH + j + 1) * NIP],
                                                    qst[0:SR, h, n * QT:(n + 1) * QT],
                                                    kipst[:, h, bass.ds(NIP * b, NIP)],
                                                    start=True, stop=True)
                elif kind == "pt":
                    pe.wait_ge(ip_probs, b + 1)
                    cols = min(128, H * NIP - 128 * i)
                    for n in range(NT):
                        last = nc.tensor.transpose(bank[0:cols, n * QT:(n + 1) * QT],
                                                   ipp[:, n, 128 * i:128 * i + cols], idf[:, :])
                elif kind == "oip":
                    if i == 0:
                        taken([("pt", 0), ("pt", 1)], which, tn)
                        pe.wait_ge(vb_made, b + 1)
                    last = nc.tensor.matmul(bank[0:TILES[i][1], :], vb[:, i, 0:TILES[i][1]], pT[:, i // 2, :],
                                            start=True, stop=True)
                elif kind == "f":
                    if i == 0 and c == 0:
                        pe.wait_ge(wo_in, 16 * ND)
                        taken([("oip", t) for t in range(ND)], which, tn)
                    last = nc.tensor.matmul(bank[:, 0:D], oT[:, c, i * QT:(i + 1) * QT], wo[:, c, :],
                                            start=(c == 0), stop=ends)
                elif kind in ("den", "num"):
                    pe.wait_ge(og_made, NG * b + i + 1)
                    pe.wait_ge(pick_made, 1)
                    last = nc.tensor.matmul(bank[64:64 + GH * DH, :], pick[:, 1 if kind == "den" else 0, :],
                                            og[:, i % 2, :], start=True, stop=True)
                elif kind == "kip":
                    pe.wait_ge(cip_in, 16)
                    pe.wait_ge(wip_in, 16)
                    for t, rows in TILES:
                        for cc in range(NC):
                            last = nc.tensor.matmul(bank[0:rows, t * B * NIP:(t + 1) * B * NIP],
                                                    wip[:, cc, 128 * t:128 * t + rows], cipT[:, cc, :],
                                                    start=(cc == 0), stop=(cc == NC - 1))
                elif kind == "vip":
                    if c == 0:
                        pe.wait_ge(wip_in, 32)
                    last = nc.tensor.matmul(bank[0:B * NIP, 0:D], cipT[:, c, :], wip[:, c, :],
                                            start=(c == 0), stop=ends)
                if ends:
                    last.then_inc(work_done, 1)

            def task(which, b, tn):
                for c in range(PIECES.get(which[0], 1)):
                    piece(which, c, b, tn)

            def st(b, s, j, wide, first_wide):
                g, kt = s // NT, s % NT
                h = g * GH + j
                i = UNITS * b + s * SLOTS + j
                if kt == 0 and j == 0:
                    pe.wait_ge(m_rows, 16 * (NG * b + g + 1))
                if first_wide and j >= 2:
                    pe.wait_ge(mx_read, UNITS * (b + 1))
                elif wide and not first_wide:
                    pe.wait_ge(exp_done, i - 3)
                elif not (isinstance(i, int) and i < 2):
                    pe.wait_ge(exp_done, i - 1)
                bank = wide_bank[j] if wide else st_bank[j % 2]
                nc.tensor.matmul(bank[0:KT, :], kst[:, h, kt * KT:(kt + 1) * KT], qst[:, h, :],
                                 start=True, stop=True).then_inc(st_done, 1)

            def mx(b, u, j):
                g, n = u // NT, u % NT
                h = g * GH + j
                i = UNITS * b + u * SLOTS + j
                if n == 0 and j == 0 and g % 2 == 0:
                    pe.wait_ge(stacked[g // 2], 16 * 2 * len(PAIRS) * (b + 1))
                if not (isinstance(i, int) and i < 2):
                    pe.wait_ge(mx_read, i - 1)
                nc.tensor.matmul(mx_bank[j % 2][:, 0:T], qst[0:SR, h, n * QT:(n + 1) * QT], kst[0:SR, h, :],
                                 start=True, stop=True).then_inc(mx_done, 1)

            def pv(b, s):
                g, kt = s // NT, s % NT
                if kt == 0:
                    pe.wait_ge(values_made, NG * b + g + 1)
                    earlier = NG * b + g - {0: 1, 1: 3}.get(g, 2)
                    if not (isinstance(earlier, int) and earlier < 0):
                        pe.wait_ge(og_made, earlier + 1)
                pe.wait_ge(exp_done, UNITS * b + (s + 1) * SLOTS)
                for j in range(GH):
                    last = nc.tensor.matmul(pv_bank[g % 2][32 * j:32 * (j + 1), :], vaug[:, kt, g * GH + j, :],
                                            P[:, s % 2, j, :], start=(kt == 0), stop=(kt == NT - 1))
                last.then_inc(pv_done, 1)

            def iteration(b, has_last, has_next):
                tn = turns(b, has_last, has_next)
                pieces = by_piece(has_last, has_next)
                for s in range(STEPS):
                    wide = not has_next and s >= WIDE
                    if not has_next and s == STEPS - 1:
                        for which in EPILOGUE[:2]:
                            task(which, b, EPI)
                    for j in range(SLOTS):
                        st(b, s, j, wide, wide and s == WIDE)
                        u = s + LEAD
                        if u < STEPS:
                            mx(b, u, j)
                        elif has_next:
                            mx(b + 1, u - STEPS, j)
                        if s * SLOTS + j in pieces:
                            which, c = pieces[s * SLOTS + j]
                            piece(which, c, batch_of(which, b), tn)
                        if j == (3 if wide else 1):
                            if s > 0:
                                pv(b, s - 1)
                            elif has_last:
                                pv(b - 1, STEPS - 1)
                if not has_next:
                    task(("oip", 0), b, EPI)
                    pv(b, STEPS - 1)

            pe.wait_ge(zeroed_v, 1)
            for _ in range(WARM_UP):
                nc.tensor.matmul(work[1][:, :], pT[:, 1, 0:128], pT[:, 1, :], start=True, stop=True)
            pe.wait_ge(zeroed_v, 5)
            pe.wait_ge(wq_in, 32)
            for which in BEFORE_MX:
                if which == ("k", 0):
                    pe.wait_ge(wk_in, 16)
                task(which, 0, PRO)
            pe.wait_ge(wv_in, 16)
            for u in range(NT):
                for j in range(SLOTS):
                    mx(0, u, j)
                    if j < NT - 1:
                        n = u * (NT - 1) + j
                        piece(("v", n // NC), n % NC, 0, PRO)
            task(("mt", 0), 0, PRO)
            for u in range(NT, LEAD):
                for j in range(SLOTS):
                    mx(0, u, j)
                    if u == NT:
                        piece(("v", NT - 1), j, 0, PRO)
            iteration(0, False, True)
            with pe.Fori(1, B - 1) as b:
                iteration(b, True, True)
            iteration(B - 1, True, False)
            task(("oip", 1), B - 1, EPI)
            pe.wait_ge(og_made, NG * B)
            pe.wait_ge(pick_made, 1)
            for c in (1, 0):
                nc.tensor.matmul(pv_bank[c][0:GH * DH, :], pick[:, c, :], og[:, (NG - 1) % 2, :],
                                 start=True, stop=True).then_inc(picked, 1)
            task(("oip", 2), B - 1, EPI)
            pe.wait_ge(mx_read, UNITS * B)
            pe.wait_ge(exp_done, UNITS * B)

            def tail_project(i, t):
                return nc.tensor.matmul(tail_bank[i][:, 0:D], oT[:, t, i * QT:(i + 1) * QT], wo[:, t, :],
                                        start=(t == 0), stop=(t == ND - 1))

            pe.wait_ge(work_free[EPI.bank(("oip", 0))], EPI.uses(("oip", 0)) + 1)
            for i in range(NT):
                tail_project(i, 0)
            pe.wait_ge(work_free[EPI.bank(("oip", 1))], EPI.uses(("oip", 1)) + 1)
            for i in range(NT):
                tail_project(i, 1)
                pe.wait_ge(tail_made, i + 1)
                tail_project(i, 2).then_inc(tail_f, 1)

        @block.scalar
        def _(act):
            def copy_out(dst, src, which, tn):
                nc.scalar.activation(dst, src, ACT.Copy).then_inc(work_free[tn.bank(which)], 1)

            def task(which, b, tn):
                kind, i = which
                if kind in ("oip", "f", "den", "num"):
                    return
                bank = work[tn.bank(which)]
                act.wait_ge(work_done, tn.done(which))
                if which in PROJ:
                    n = PROJ.index(which)
                    if not (isinstance(b, int) and b == 0):
                        act.wait_ge(parts_out[n], 16 * b)
                    nc.scalar.activation(parts[:, n, 0, :], bank[:, :], ACT.Copy).then_inc(first_part, 1)
                elif kind == "v":
                    if i == 0 and not (isinstance(b, int) and b == 0):
                        act.wait_ge(values_made, NG * b)
                    copy_out(vst[:, i, :], bank[0:KT, 0:D], which, tn)
                elif kind == "mt":
                    n = NG * b + i
                    if not (isinstance(n, int) and n == 0):
                        act.wait_ge(m_rows, 16 * n)
                    copy_out(mT[:, :], bank[0:3 * GH * NT, 0:128], which, tn)
                elif kind in ("ips", "ips_first"):
                    if not (isinstance(b, int) and b == 0):
                        act.wait_ge(ip_masked, b)
                    nc.scalar.activation(ips[:, :, i * GH * NIP:(i + 1) * GH * NIP],
                                         bank[:, 0:NT * GH * NIP].rearrange("p (n c) -> p n c", n=NT),
                                         ACT.Copy, scale=SCALE).then_inc(work_free[tn.bank(which)], 1)
                elif kind == "pt":
                    cols = min(128, H * NIP - 128 * i)
                    copy_out(pT[0:cols, i, :], bank[0:cols, :], which, tn)
                elif kind == "kip":
                    for t, rows in TILES:
                        nc.scalar.activation(kipp[0:rows, 0, t], bank[0:rows, t * B * NIP:(t + 1) * B * NIP],
                                             ACT.Copy).then_inc(kip_first, 1)
                elif kind == "vip":
                    copy_out(vips[:, :], bank[0:B * NIP, 0:D], which, tn)

            def exp(b, s, j, wide):
                i = UNITS * b + s * SLOTS + j
                act.wait_ge(st_done, i + 1)
                step = STEPS * b + s
                if j == 0 and not (isinstance(step, int) and step < 2):
                    act.wait_ge(pv_done, step - 1)
                bank = wide_bank[j] if wide else st_bank[j % 2]
                nc.scalar.activation(P[:, s % 2, j, :], bank[0:KT, :], ACT.Exp,
                                     scale=SCALE).then_inc(exp_done, 1)

            def take_output(b, g):
                n = NG * b + g
                act.wait_ge(pv_done, NT * (n + 1))
                earlier = n - {0: 1, 1: 3}.get(g, 2)
                if not (isinstance(earlier, int) and earlier < 0):
                    act.wait_ge(og_out, 16 * (earlier + 1))
                nc.scalar.activation(og[:, g % 2, :], pv_bank[g % 2][:, :], ACT.Copy).then_inc(og_made, 1)

            def iteration(b, has_last, has_next):
                tn = turns(b, has_last, has_next)
                tasks = by_end(has_last, has_next)
                for s in range(STEPS):
                    wide = not has_next and s >= WIDE
                    for j in range(SLOTS):
                        exp(b, s, j, wide)
                        if s * SLOTS + j in tasks:
                            which = tasks[s * SLOTS + j]
                            task(which, batch_of(which, b), tn)
                        if j == (3 if wide else 2) and s % NT == 0:
                            if s > 0:
                                take_output(b, s // NT - 1)
                            elif has_last:
                                take_output(b - 1, NG - 1)
                        if (s, j) == ((17, 0) if has_next else (16, 0)):
                            act.wait_ge(ip_shifted, b + 1)
                            nc.scalar.activation(ipp[:, :, :], ipp[:, :, :], ACT.Exp).then_inc(ip_exp, 1)
                if not has_next:
                    take_output(b, NG - 1)

            act.dma_start(wk[:, :, :], w_k.rearrange("(c p) d -> p c d", p=128)).then_inc(wk_in, 16)
            act.dma_start(boxes[:, :, :, :].rearrange("p b m c -> p (b m c)"),
                          bbox.rearrange("b m c -> (b m c)").unsqueeze(0).broadcast_to([128, B * 16])).then_inc(box_in, 16)
            act.dma_start(gxy[:, :, :], grid.rearrange("(n p) c -> p n c", p=QT)).then_inc(box_in, 16)
            act.wait_ge(c_in, 16)
            act.dma_start(wip[:, :, :], w_k_ip.rearrange("(c p) d -> p c d", p=128)).then_inc(wip_in, 16)
            act.dma_start(wv[:, :, :], w_v.rearrange("(c p) d -> p c d", p=128)).then_inc(wv_in, 16)
            for which in PROLOGUE:
                task(which, 0, PRO)
                if which == ("v", 0):
                    act.dma_start(wip[:, :, :], w_v_ip.rearrange("(c p) d -> p c d", p=128)).then_inc(wip_in, 16)
            iteration(0, False, True)
            with act.Fori(1, B - 1) as b:
                iteration(b, True, True)
            iteration(B - 1, True, False)

        @block.vector
        def _(dve):
            def task(which, b, tn):
                kind, i = which
                if kind not in ("q", "k", "qk", "oip", "f", "kip", "den", "num") and not (kind == "pt" and tn is EPI):
                    return
                bank = work[tn.bank(which)]
                free = work_free[tn.bank(which)]
                if which in PROJ:
                    p = PROJ.index(which)
                    n = NP * b + p
                    dve.wait_ge(first_part, n + 1)
                    if not (isinstance(n, int) and n < 2):
                        dve.wait_ge(parts_made, n if p == 0 else n - 1)
                    nc.vector.tensor_tensor(resid[:, p % 2, :], bank[:, :], parts[:, p, 0, :],
                                            ALU.subtract).then_inc(free, 1)
                    dve.wait_ge(free, tn.uses(which) + 1)
                    nc.vector.tensor_copy(parts[:, p, 1, :], resid[:, p % 2, :]).then_inc(second_part, 1)
                    if tn is PRO and p < 2:
                        dve.wait_ge(second_part, n + 1)
                        nc.vector.tensor_tensor(parts[:, p, 2, :], resid[:, p % 2, :], parts[:, p, 1, :],
                                                ALU.subtract).then_inc(parts_made, 1)
                elif kind == "oip":
                    rows = TILES[i][1]
                    dve.wait_ge(work_done, tn.done(which))
                    dve.wait_ge(normed, ND * b + i + 1)
                    nc.vector.tensor_tensor(oT[0:rows, i, :], bank[0:rows, :], num[0:rows, i, :],
                                            ALU.add).then_inc(free, 1)
                elif kind == "f":
                    dve.wait_ge(work_done, tn.done(which))
                    if i == 0:
                        dve.wait_ge(res_made, b + 1)
                    nc.vector.tensor_tensor(ob[:, i, :], bank[:, 0:D], xres[:, i, :], ALU.add).then_inc(free, 1)
                elif kind == "pt":
                    dve.wait_ge(work_done, tn.done(which))
                    cols = min(128, H * NIP - 128 * i)
                    nc.vector.tensor_copy(pT[0:cols, i, :], bank[0:cols, :]).then_inc(free, 1)
                elif kind == "den":
                    dve.wait_ge(work_done, tn.done(which))
                    nc.vector.reciprocal(tail_inv[64:128, :], bank[64:128, :]).then_inc(free, 1)
                elif kind == "num":
                    dve.wait_ge(work_done, tn.done(which))
                    before = ("den", i)
                    dve.wait_ge(work_free[tn.bank(before)], tn.uses(before) + 1)
                    nc.vector.tensor_tensor(num[64:128, i // 2, :], bank[64:128, :], tail_inv[64:128, :],
                                            ALU.mult).then_inc(free, 1)
                elif kind == "kip":
                    w = B * NIP
                    dve.wait_ge(kip_first, ND)
                    for t, rows in TILES:
                        nc.vector.tensor_tensor(kipr[0:rows, t], bank[0:rows, t * w:(t + 1) * w],
                                                kipp[0:rows, 0, t], ALU.subtract).then_inc(kip_step, 1)
                    dve.wait_ge(kip_step, ND)
                    for t, rows in TILES:
                        nc.vector.tensor_copy(kipp[0:rows, 1, t], kipr[0:rows, t]).then_inc(kip_step, 1)
                    dve.wait_ge(kip_step, 2 * ND)
                    for t, rows in TILES:
                        last = nc.vector.tensor_tensor(kipp[0:rows, 2, t], kipr[0:rows, t], kipp[0:rows, 1, t], ALU.subtract)
                        if t < ND - 1:
                            last.then_inc(kip_step, 1)
                    last.then_inc(kip_parts, 1)
                    dve.wait_ge(kip_parts, 1)
                    nc.vector.memset(kipr[0:1, 0, 0:1], 0.0).then_inc(free, 1)

            def row_max(b, u, j):
                n = u % NT
                i = UNITS * b + u * SLOTS + j
                dve.wait_ge(mx_done, i + 1)
                nc.vector.tensor_reduce(mrow[:, j * NT + n:j * NT + n + 1], mx_bank[j % 2][:, 0:T],
                                        axis=AX.X, op=ALU.max).then_inc(mx_read, 1)

            def cut_maxima(b, g):
                n = NG * b + g
                w = GH * NT
                dve.wait_ge(mx_read, UNITS * b + (g + 1) * NT * SLOTS)
                nc.vector.tensor_scalar(mparts[:, 0:w], mrow[:, :], -1.0, None, ALU.mult).then_inc(m_step, 1)
                dve.wait_ge(m_step, 3 * n + 1)
                nc.vector.scalar_tensor_tensor(out=mres[:, :], in0=mrow[:, :], scalar=-1.0, in1=mparts[:, 0:w],
                                               op0=ALU.mult, op1=ALU.subtract).then_inc(m_step, 1)
                dve.wait_ge(m_step, 3 * n + 2)
                nc.vector.tensor_copy(mparts[:, w:2 * w], mres[:, :]).then_inc(m_step, 1)
                dve.wait_ge(m_step, 3 * n + 3)
                nc.vector.tensor_tensor(mparts[:, 2 * w:3 * w], mres[:, :], mparts[:, w:2 * w],
                                        ALU.subtract).then_inc(m_parts, 1)

            def lay_values(b, g, tn):
                if g == 0:
                    for i in (NT - 2, NT - 1):
                        dve.wait_ge(work_free[tn.bank(("v", i))], tn.uses(("v", i)) + 1)
                if isinstance(b, int) and b == 0:
                    dve.wait_ge(zeroed_p, 4)
                else:
                    dve.wait_ge(pv_done, STEPS * (b - 1) + NT * (g + 1))
                nc.vector.tensor_copy(
                    vaug[:, :, g * GH:(g + 1) * GH, 0:DH],
                    vst[:, :, g * GH * DH:(g + 1) * GH * DH].rearrange("p n (h d) -> p n h d", d=DH)).then_inc(values_made, 1)

            def invert_den(b, g):
                a_batch = NG // 2 + 1 if g % 2 == 0 else NG // 2
                dve.wait_ge(den_in[g % 2], 16 * (a_batch * b + g // 2 + 1))
                nc.vector.reciprocal(denc[:, g % 2, :], denc[:, g % 2, :]).then_inc(den_inv, 1)

            LAY = {(16, 2): 0, (17, 0): 1, (17, 2): 2, (18, 3): 3}

            def iteration(b, has_last, has_next):
                tn = turns(b, has_last, has_next)
                tasks = by_end(has_last, has_next)
                for s in range(STEPS):
                    for j in range(SLOTS):
                        u = s + LEAD
                        if u < STEPS:
                            row_max(b, u, j)
                        elif has_next:
                            row_max(b + 1, u - STEPS, j)
                        if j == SLOTS - 1 and s % NT == 1:
                            if u < STEPS:
                                cut_maxima(b, u // NT)
                            elif has_next:
                                cut_maxima(b + 1, u // NT - NG)
                        if s * SLOTS + j in tasks:
                            which = tasks[s * SLOTS + j]
                            task(which, batch_of(which, b), tn)
                        if (s, j) == (1, 0) and has_last:
                            lay_values(b, NG - 1, None)
                        if has_next and (s, j) in LAY:
                            lay_values(b + 1, LAY[s, j], tn)
                        if (s, j) == (2, 3) and has_last:
                            invert_den(b - 1, NG - 1)
                        if s > 4 and (s % NT, j) == (0, 2) and (has_next or s < 16):
                            invert_den(b, s // NT - 2)
                        if (s, j) == (15, 2) and not has_next:
                            invert_den(b, 2)
                        if (s, j) == (0, 3) and has_last:
                            invert_den(b - 1, NG - 2)
                        if (s, j) == ((16, 0) if has_next else (14, 2)):
                            dve.wait_ge(ip_masked, b + 1)
                            nc.vector.tensor_reduce(ipmax[:, :], ipp[:, :, :].rearrange("p n (h k) -> p (n h) k", k=NIP),
                                                    axis=AX.X, op=ALU.max).then_inc(ip_max, 1)
                        if (s, j) == ((18, 0) if has_next else (16, 2)):
                            dve.wait_ge(ip_exp, b + 1)
                            nc.vector.tensor_reduce(ipden[:, :], ipp[:, :, :].rearrange("p n (h k) -> p (n h) k", k=NIP),
                                                    axis=AX.X, op=ALU.add).then_inc(ip_step, 1)
                        if (s, j) == ((19, 1) if has_next else (17, 0)):
                            dve.wait_ge(ip_step, b + 1)
                            nc.vector.reciprocal(ipden[:, :], ipden[:, :]).then_inc(ip_inv, 1)

            nc.vector.memset(pT[:, 1, :], 0.0).then_inc(zeroed_v, 1)
            for padded in (xT, wq, wo, oT):
                nc.vector.memset(padded[TILES[-1][1]:128, ND - 1, :], 0.0).then_inc(zeroed_v, 1)
            dve.wait_ge(box_in, 32)
            for e, (corner, axis, op) in enumerate(((0, 0, ALU.is_ge), (1, 1, ALU.is_ge), (2, 0, ALU.is_le), (3, 1, ALU.is_le))):
                for b in range(B):
                    nc.vector.tensor_tensor(
                        compared[:, e, 16 * b:16 * (b + 1)].rearrange("p (n m) -> p n m", n=NT),
                        gxy[:, :, axis:axis + 1].broadcast_to([128, NT, 4]),
                        boxes[:, b, :, corner].unsqueeze(1).broadcast_to([128, NT, 4]), op).then_inc(box_step, 1)
            dve.wait_ge(box_step, 4 * B)
            nc.vector.tensor_tensor(compared[:, 0], compared[:, 0], compared[:, 1], ALU.mult).then_inc(box_step, 1)
            nc.vector.tensor_tensor(compared[:, 2], compared[:, 2], compared[:, 3], ALU.mult).then_inc(box_step, 1)
            dve.wait_ge(box_step, 4 * B + 2)
            nc.vector.tensor_tensor(compared[:, 0], compared[:, 0], compared[:, 2], ALU.mult).then_inc(box_step, 1)
            dve.wait_ge(box_step, 4 * B + 3)
            inside = compared[:, 0].rearrange("p (n m) -> p n m", m=4)
            nc.vector.tensor_reduce(anyin[:, :], inside, axis=AX.X, op=ALU.max).then_inc(box_step, 1)
            mask_rows = mask[:, :, :, :].rearrange("p b n k -> p (b n) k")
            nc.vector.tensor_scalar(mask_rows[:, :, 4:8], inside, 1.0, -NEG, ALU.subtract, ALU.mult).then_inc(mask_made, 1)
            dve.wait_ge(box_step, 4 * B + 4)
            nc.vector.tensor_scalar(mask_rows[:, :, 0:4], anyin[:, :].unsqueeze(2).broadcast_to([128, B * NT, 4]),
                                    NEG, None, ALU.mult).then_inc(mask_made, 1)
            for which in BEFORE_MX:
                task(which, 0, PRO)
            dve.wait_ge(eye_in, 16)
            nc.vector.tensor_copy(idb[:, :], idf[:, :]).then_inc(idb_made, 1)
            nc.vector.tensor_copy(pick[:, :, :].rearrange("p c (j d) -> p c j d", j=GH),
                                  idf[:, :].rearrange("p (j c d) -> p c j d", c=2, d=DH)).then_inc(pick_made, 1)
            for u in range(NT):
                for j in range(SLOTS):
                    row_max(0, u, j)
            cut_maxima(0, 0)
            for u in range(NT, LEAD):
                for j in range(SLOTS):
                    row_max(0, u, j)
            for g in range(NG):
                lay_values(0, g, PRO)
            iteration(0, False, True)
            with dve.Fori(1, B - 1) as b:
                iteration(b, True, True)
            iteration(B - 1, True, False)

            def tail_invert(i):
                q = slice(i * QT, (i + 1) * QT)
                nc.vector.reciprocal(tail_inv[0:rows, q], pv_bank[1][0:rows, q]).then_inc(tail_inverted, 1)

            def tail_heads(i):
                q = slice(i * QT, (i + 1) * QT)
                dve.wait_ge(tail_inverted, i + 1)
                nc.vector.tensor_tensor(tail_num[0:rows, q], pv_bank[0][0:rows, q], tail_inv[0:rows, q],
                                        ALU.mult).then_inc(tail_normed, 1)
                dve.wait_ge(tail_normed, i + 1)
                nc.vector.tensor_tensor(oT[0:rows, ND - 1, q], work[EPI.bank(("oip", ND - 1))][0:rows, q],
                                        tail_num[0:rows, q], ALU.add).then_inc(tail_made, 1)

            def tail_output(i):
                dve.wait_ge(tail_f, i + 1)
                nc.vector.tensor_tensor(ob[:, i, :], tail_bank[i][:, 0:D], xres[:, i, :], ALU.add).then_inc(tail_ob, 1)

            rows = GH * DH
            task(("pt", 0), B - 1, EPI)
            task(("pt", 1), B - 1, EPI)
            dve.wait_ge(work_free[END.bank(("num", NG - 2))], END.uses(("num", NG - 2)) + 1)
            task(("oip", 0), B - 1, EPI)
            task(("oip", 1), B - 1, EPI)
            dve.wait_ge(picked, 1)
            tail_invert(0)
            dve.wait_ge(picked, 2)
            dve.wait_ge(work_done, EPI.done(("oip", ND - 1)))
            tail_heads(0)
            tail_invert(1)
            tail_heads(1)
            tail_invert(2)
            dve.wait_ge(res_made, B)
            tail_output(0)
            tail_heads(2)
            tail_invert(3)
            tail_output(1)
            tail_heads(3)
            tail_output(2)
            tail_output(3)

        @block.gpsimd
        def _(pool):
            def cut(p, b, tn):
                n = NP * b + p
                pool.wait_ge(second_part, n + 1)
                if not (isinstance(b, int) and b == 0):
                    pool.wait_ge(parts_out[p], 16 * b)
                nc.gpsimd.tensor_tensor(out=parts[:, p, 2, :], in0=resid[:, p % 2, :], in1=parts[:, p, 1, :],
                                        op=ALU.subtract).then_inc(parts_made, 1)

            def normalise(b, t):
                rows = TILES[t][1]
                pool.wait_ge(placed[t], (b + 1) * (64 if t < 2 else 32))
                nc.gpsimd.tensor_tensor(out=num[0:rows, t], in0=num[0:rows, t], in1=den[0:rows, t],
                                        op=ALU.mult).then_inc(normed, 1)

            def add_bias(b):
                pool.wait_ge(xres_in, 16 * (b + 1))
                nc.gpsimd.tensor_tensor(out=xres[:, :, :], in0=xres[:, :, :],
                                        in1=bias[:, :].unsqueeze(1).broadcast_to([128, NT, D]),
                                        op=ALU.add).then_inc(res_made, 1)

            heads = ipp[:, :, :].rearrange("p n (h k) -> p (n h) k", k=NIP)

            def mask_scores(b, tn):
                pool.wait_ge(work_free[tn.bank(("ips", 4))], tn.uses(("ips", 4)) + 1)
                if tn.has(("pt", 1)):
                    pool.wait_ge(work_done, tn.done(("pt", 1)))
                for n in range(NT):
                    last = nc.gpsimd.tensor_tensor(
                        out=ipp[:, n].rearrange("p (h k) -> p h k", k=NIP),
                        in0=ips[:, n].rearrange("p (h k) -> p h k", k=NIP),
                        in1=mask[:, b, n, :].unsqueeze(1).broadcast_to([128, H, NIP]), op=ALU.add)
                last.then_inc(ip_masked, 1)

            def shift(b):
                pool.wait_ge(ip_max, b + 1)
                nc.gpsimd.tensor_tensor(out=heads, in0=heads, in1=ipmax[:, :].unsqueeze(2).broadcast_to([128, NT * H, NIP]),
                                        op=ALU.subtract).then_inc(ip_shifted, 1)

            def probabilities(b):
                pool.wait_ge(ip_inv, b + 1)
                nc.gpsimd.tensor_tensor(out=heads, in0=heads, in1=ipden[:, :].unsqueeze(2).broadcast_to([128, NT * H, NIP]),
                                        op=ALU.mult).then_inc(ip_probs, 1)

            def lay_ip_values(b, tn):
                if isinstance(b, int) and b == 0:
                    pool.wait_ge(vblocks_in, 16 * H)
                if tn.has(("oip", 2)):
                    pool.wait_ge(work_done, tn.done(("oip", 2)))
                nc.gpsimd.tensor_copy(vb[:, :, :], vblocks[:, b, :, :]).then_inc(vb_made, 1)

            def iteration(b, has_last, has_next):
                tn = turns(b, has_last, has_next)
                if has_last:
                    if not has_next:
                        normalise(b - 1, 2)
                        add_bias(b - 1)
                if has_next:
                    for p in range(NP):
                        cut(p, b + 1, tn)
                        if p == 1 and has_last:
                            normalise(b - 1, 2)
                        if p == 2 and has_last:
                            add_bias(b - 1)
                if has_next:
                    normalise(b, 0)
                    mask_scores(b, tn)
                else:
                    mask_scores(b, tn)
                    normalise(b, 0)
                    lay_ip_values(b, tn)
                shift(b)
                probabilities(b)
                if has_next:
                    normalise(b, 1)
                    lay_ip_values(b, tn)
                else:
                    pool.wait_ge(placed[1], 64 * (b + 1) - 32)
                    nc.gpsimd.tensor_tensor(out=num[0:GH * DH, 1], in0=num[0:GH * DH, 1], in1=den[0:GH * DH, 1],
                                            op=ALU.mult).then_inc(normed, 1)
                    add_bias(b)


            pair_of_ones = 1.0 + 0x3F80 / 2.0 ** 23
            nc.gpsimd.memset(qst[96:128, :, :].rearrange("p h s -> p (h s)").bitcast(fp32), 0.0).then_inc(zeroed_p, 1)
            nc.gpsimd.memset(kst[96:128, :, :].rearrange("p h s -> p (h s)").bitcast(fp32), pair_of_ones).then_inc(zeroed_p, 1)
            pool.wait_ge(zeroed_p, 2)
            nc.gpsimd.memset(vblocks[:, :, :, :].rearrange("p b t c -> p (b t c)"), 0.0).then_inc(zeroed_p, 1)
            pool.wait_ge(zeroed_p, 3)
            nc.gpsimd.memset(vaug[:, :, :, :].rearrange("p n h c -> p (n h c)"), 1.0).then_inc(zeroed_p, 1)
            pool.wait_ge(zeroed_p, 4)
            for p in range(2, NP):
                cut(p, 0, PRO)
            pool.wait_ge(bias_in, 16)
            pool.wait_ge(mask_made, 2)
            iteration(0, False, True)
            with pool.Fori(1, B - 1) as b:
                iteration(b, True, True)
            iteration(B - 1, True, False)


_INS = ['fside_Bx4x4_0', 'L0_xattn_w_q', 'L0_xattn_w_k', 'L0_xattn_w_v',
        'L0_xattn_w_k_ip', 'L0_xattn_w_v_ip', 'L0_xattn_w_out', 'L0_xattn_b_out']


def kernel(**inputs):
    import numpy as _np
    import concourse.bacc as _bacc
    from concourse import mybir as _mybir
    from concourse.bass_utils import run_bass_kernel_spmd as _run

    nc = _bacc.Bacc("TRN2", target_bir_lowering=False, num_devices=1)
    arrays, args = {}, []

    def give(name, a):
        arrays[name] = a
        args.append(nc.dram_tensor(name, a.shape, _mybir.dt.from_np(a.dtype), kind="ExternalInput").ap())

    text = inputs['ctx_2048'].shape[1] - 8
    give("in_x_dram", _np.ascontiguousarray(inputs['x']))
    give("in_x_t_dram", _np.ascontiguousarray(_np.transpose(inputs['x'], (0, 2, 1))))
    give("in_ctx_t_dram", _np.ascontiguousarray(_np.transpose(inputs['ctx_2048'], (0, 2, 1))))
    give("in_ctx_ip_t_dram", _np.ascontiguousarray(
        _np.transpose(inputs['ctx_2048'][:, text:], (2, 0, 1))).reshape(inputs['ctx_2048'].shape[2], -1))
    for name in _INS:
        give(f"in_{name}_dram", _np.ascontiguousarray(inputs[name]))
    seq = inputs['x'].shape[1]
    width = next(w for w in range(int(seq ** 0.5), seq + 1) if seq % w == 0)

    def line(n):
        c = _np.arange(n, dtype=_np.float32) * (_np.float32(1) / _np.float32(n - 1))
        c[-1] = 1
        return c
    pos = _np.arange(seq)
    grid = _np.stack([line(width)[pos % width], line(seq // width)[pos // width]], axis=1)
    give("grid_dram", _np.ascontiguousarray(grid))
    give("eye_dram", _np.eye(128, dtype=_np.float32))
    shape = tuple(inputs['x'].shape)
    args.append(nc.dram_tensor("out_0_dram", shape, _mybir.dt.float32, kind="ExternalOutput").ap())
    cross_attention_kernel(nc, *args)
    r = _run(nc, [arrays], core_ids=[0])
    return r.results[0]["out_0_dram"]
```
